# Optimizing a Trainium2 kernel written in Bass

```python
import numpy as np
import jax
import jax.numpy as jnp

def _softmax(x, axis=-1):
    return jax.nn.softmax(x, axis=axis)
def _gelu(x):
    return jax.nn.gelu(x, approximate=True)
def _silu(x):
    return jax.nn.silu(x)
def _sigmoid(x):
    return jax.nn.sigmoid(x)
def _layernorm(x, axis=-1, eps=1e-5):
    m = jnp.mean(x, axis=axis, keepdims=True)
    v = jnp.var(x, axis=axis, keepdims=True)
    return (x - m) / jnp.sqrt(v + eps)
def _scatter_add(tgt, idx, src, axis=0):
    return tgt.at[idx].add(src)
def _segment_sum(src, seg, n):
    return jax.ops.segment_sum(src, seg, n)

kernel_name = 'mk_adj_resnorm_d2_adj_64_ac3c1c'

def setup_inputs(seed: int = 0):
    np.random.seed(seed)
    _w = jnp.asarray
    def _rec_inputs():
        import jax
        import jax.numpy as jnp
        _gk = jax.random.key(seed)
        x = 0.0002141 + 1 * jax.random.normal(jax.random.fold_in(_gk, 1), (4096, 64), jnp.float32)
        _w = (1.0 + jnp.arange(4096, dtype=jnp.float32)) ** -0.5
        _w = _w / _w.mean()
        _pij = jnp.clip(0.000976562 * _w[:, None] * _w[None, :], 0.0, 1.0)
        _a = jax.random.uniform(jax.random.fold_in(_gk, 2), (4096, 4096)) < _pij
        _a = jnp.logical_or(_a, jnp.eye(4096, dtype=bool))
        _af = _a.astype(jnp.float32)
        _af = _af * jax.random.uniform(jax.random.fold_in(_gk, 3), (4096, 4096), jnp.float32, 0.05, 1)
        adj = _af
        return x, adj
    x, adj = _rec_inputs()
    def _L0_gnn_setup():
        import jax, jax.numpy as jnp
        import numpy as np
        N, D = (12288, 64)

        def _ggc(x, adj, W, wih, whh, bih, bhh):
            m = adj @ (x @ W)
            gi = m @ wih.T + bih
            gh = x @ whh.T + bhh
            i_r, i_z, i_n = jnp.split(gi, 3, axis=-1)
            h_r, h_z, h_n = jnp.split(gh, 3, axis=-1)
            r = jax.nn.sigmoid(i_r + h_r)
            z = jax.nn.sigmoid(i_z + h_z)
            n = jnp.tanh(i_n + r * h_n)
            return (1.0 - z) * n + z * x
        key = jax.random.key(seed)
        ks = jax.random.split(key, 8)
        s = 1.0 / np.sqrt(D)
        return {'x': jax.random.normal(ks[0], (N, D), jnp.float32), 'adj': jax.random.uniform(ks[1], (N, N), jnp.float32), 'W1': jax.random.normal(ks[2], (D, D), jnp.float32) * s, 'wih1': jax.random.normal(ks[3], (3 * D, D), jnp.float32) * s, 'whh1': jax.random.normal(ks[4], (3 * D, D), jnp.float32) * s, 'bih1': jnp.zeros((3 * D,), jnp.float32), 'bhh1': jnp.zeros((3 * D,), jnp.float32), 'W2': jax.random.normal(ks[5], (D, D), jnp.float32) * s, 'wih2': jax.random.normal(ks[6], (3 * D, D), jnp.float32) * s, 'whh2': jax.random.normal(ks[7], (3 * D, D), jnp.float32) * s, 'bih2': jnp.zeros((3 * D,), jnp.float32), 'bhh2': jnp.zeros((3 * D,), jnp.float32)}
    _L0_gnn_all = _L0_gnn_setup()
    _L0_gnn_in = {k: v for k, v in _L0_gnn_all.items() if k in ('W1', 'wih1', 'whh1', 'bih1', 'bhh1', 'W2', 'wih2', 'whh2', 'bih2', 'bhh2', )}
    del _L0_gnn_all

    def _L1_gnn_setup():
        import jax, jax.numpy as jnp
        import numpy as np
        N, D_IN, D_OUT = (8192, 64, 64)
        MAX_NEIGH = 100
        DECAY = 0.5
        key = jax.random.key(seed)
        k1, k2, k3, k4 = jax.random.split(key, 4)
        stdv = 1.0 / np.sqrt(D_OUT)
        inputs = {'input': jax.random.normal(k1, (N, D_IN), dtype=jnp.float32), 'adj': jax.random.randint(k2, (N, N), 0, 2).astype(jnp.float32), 'weight': jax.random.uniform(k3, (D_IN, D_OUT), minval=-stdv, maxval=stdv, dtype=jnp.float32), 'bias': jax.random.uniform(k4, (D_OUT,), minval=-stdv, maxval=stdv, dtype=jnp.float32)}
        return inputs
    _L1_gnn_all = _L1_gnn_setup()
    _L1_gnn_in = {k: v for k, v in _L1_gnn_all.items() if k in ('weight', 'bias', )}
    del _L1_gnn_all

    return {
        "x": x,
        "adj": adj,
        "L0_gnn_W1": _L0_gnn_in["W1"],
        "L0_gnn_wih1": _L0_gnn_in["wih1"],
        "L0_gnn_whh1": _L0_gnn_in["whh1"],
        "L0_gnn_bih1": _L0_gnn_in["bih1"],
        "L0_gnn_bhh1": _L0_gnn_in["bhh1"],
        "L0_gnn_W2": _L0_gnn_in["W2"],
        "L0_gnn_wih2": _L0_gnn_in["wih2"],
        "L0_gnn_whh2": _L0_gnn_in["whh2"],
        "L0_gnn_bih2": _L0_gnn_in["bih2"],
        "L0_gnn_bhh2": _L0_gnn_in["bhh2"],
        "L1_gnn_weight": _L1_gnn_in["weight"],
        "L1_gnn_bias": _L1_gnn_in["bias"],
    }

def reference(x, adj, L0_gnn_W1, L0_gnn_wih1, L0_gnn_whh1, L0_gnn_bih1, L0_gnn_bhh1, L0_gnn_W2, L0_gnn_wih2, L0_gnn_whh2, L0_gnn_bih2, L0_gnn_bhh2, L1_gnn_weight, L1_gnn_bias):
    import jax
    import jax.numpy as jnp
    def _L0_gnn_ref(x, adj, W1, wih1, whh1, bih1, bhh1, W2, wih2, whh2, bih2, bhh2):
        import jax, jax.numpy as jnp
        import numpy as np
        N, D = (12288, 64)

        def _ggc(x, adj, W, wih, whh, bih, bhh):
            m = adj @ (x @ W)
            gi = m @ wih.T + bih
            gh = x @ whh.T + bhh
            i_r, i_z, i_n = jnp.split(gi, 3, axis=-1)
            h_r, h_z, h_n = jnp.split(gh, 3, axis=-1)
            r = jax.nn.sigmoid(i_r + h_r)
            z = jax.nn.sigmoid(i_z + h_z)
            n = jnp.tanh(i_n + r * h_n)
            return (1.0 - z) * n + z * x
        h = jax.nn.relu(_ggc(x, adj, W1, wih1, whh1, bih1, bhh1))
        return jax.nn.relu(_ggc(h, adj, W2, wih2, whh2, bih2, bhh2))

    def _L1_gnn_ref(input, adj, weight, bias):
        import jax, jax.numpy as jnp
        import numpy as np
        N, D_IN, D_OUT = (8192, 64, 64)
        MAX_NEIGH = 100
        DECAY = 0.5
        support = input @ weight
        mask = (adj != 0).astype(support.dtype)
        rank = jnp.cumsum(mask, axis=1)
        deg = rank[:, -1:]
        k = jnp.minimum(deg, float(MAX_NEIGH))
        pos = rank - (deg - k)
        w = mask * jnp.where(pos > 0, DECAY ** (k - pos), 0.0)
        out = w @ support + bias
        return out

    x = _layernorm(x + _L0_gnn_ref(x, adj, L0_gnn_W1, L0_gnn_wih1, L0_gnn_whh1, L0_gnn_bih1, L0_gnn_bhh1, L0_gnn_W2, L0_gnn_wih2, L0_gnn_whh2, L0_gnn_bih2, L0_gnn_bhh2), axis=-1)
    x = _layernorm(x + _L1_gnn_ref(x, adj, L1_gnn_weight, L1_gnn_bias), axis=-1)
    return x


_drawn_inputs = setup_inputs


def setup_inputs(seed=0):
    import zlib

    import numpy as np

    out = dict(_drawn_inputs(seed))
    spreads = {'L0_gnn_bih1': (0.0, 0.391),
     'L0_gnn_bhh1': (0.0, 0.636),
     'L0_gnn_bih2': (0.0, 0.1),
     'L0_gnn_bhh2': (0.0, 0.377)}
    factors = {}
    for name, (base, spread) in spreads.items():
        noise = np.random.default_rng([zlib.crc32(name.encode()), seed]).standard_normal(out[name].shape)
        drawn = base * np.exp(spread * noise) if base else spread * noise
        out[name] = jnp.asarray(drawn.astype(out[name].dtype))
    for name, factor in factors.items():
        out[name] = (out[name] * factor).astype(out[name].dtype)
    return out
```

```python
from contextlib import ExitStack

import concourse.bass as bass
from concourse import mybir

F32 = mybir.dt.float32
BF16 = mybir.dt.bfloat16
F16 = mybir.dt.float16
U8 = mybir.dt.uint8
U16 = mybir.dt.uint16
I32 = mybir.dt.int32
ALU = mybir.AluOpType
ACT = mybir.ActivationFunctionType
AX_X = mybir.AxisListType.X

P = 128
N = 4096
D = 64
CW = 512
NCH = N // CW
KT = CW // P
NT = N // P
NP = NT // 2
PW = 2 * CW
SLOTS = 8
RING = 4
NEIGH = 100
BIG = 128
CODE_SHIFT = 27
EXP_ONE = 1 << 23
EPS = 1e-5
RSUMS = 2 * (NP - 1)

Q_GATES, Q_SIG, Q_T, Q_TANH, Q_H, Q_RELU = 1, 1, 2, 3, 4, 5
Q_NODE, Q_NODE_OUT = 6, 7
Q_X1T, Q_SUP, Q_SPLIT = 9, 10, 10
BLOCKS_LAG1 = {12: 0, 13: 1, 14: 2, 15: 3}
BLOCKS_LAG2 = {0: 4, 2: 5, 3: 6, 4: 7}


def build(nc, adj_t, x_t, x, w1, w2, wih1_t, whh1_t, wih2_t, whh2_t, bih1, bhh1, bih2, bhh2,
          weight_t, bias, out, h_dram):
    with ExitStack() as ctx:
        def sb(name, shape, dt):
            return ctx.enter_context(nc.sbuf_tensor(name, shape, dt))

        def sem(name):
            return ctx.enter_context(nc.semaphore(name))

        codes = sb("codes", [P, NCH * NT * CW], U8)
        x_t_sb = codes[0:D, (NCH - 1) * NT * CW:].bitcast(F32)
        stream = sb("stream", [P, SLOTS, PW], F32)
        s_in = sb("s_in", [P, NT * D], F32)
        x1b = s_in
        s_mid = sb("s_mid", [P, NT * D], F32)
        shared = sb("shared", [P, NCH * CW], F32)
        out_acc = shared[:, :]
        masks = shared[:, 0:RING * CW].bitcast(BF16)
        rsums = shared[:, RING * CW:2 * RING * CW].bitcast(BF16)
        wexp = sb("wexp", [P, 2, KT * CW], BF16)
        mx = sb("mx", [P, CW], F32)
        m_high_t = sb("m_high_t", [P, CW], F32)
        m_high = m_high_t[0:D, :]
        t_n = m_high_t[D:P, :]
        rz = sb("rz", [P, CW], F32)
        x1_t_n = sb("x1_t_n", [P, CW], F32)
        x1_t = x1_t_n[0:D, :]
        n_g = x1_t_n[D:P, :]
        h_c = sb("h_c", [P, CW], F32)
        x_n = sb("x_n", [P, KT, D], F32)
        y = sb("y", [P, KT, D], F32)
        sq = sb("sq", [P, KT, D], F32)
        x1 = sb("x1", [P, KT, D], F32)
        o_n = sb("o_n", [P, 2, KT, D], F32)
        stat = sb("stat", [P, 5, KT], F32)
        mhalf = sb("mhalf", [P, KT], F32)
        sup = sb("sup", [P, KT, 2, D], F16)
        w_rz = [sb(f"w_rz{i}", [P, P], F32) for i in range(2)]
        w_n = [sb(f"w_n{i}", [P, P], F32) for i in range(2)]
        w12 = sb("w12", [P, D], F32)
        b_i = sb("b_i", [P, 2], F32)
        b_h = sb("b_h", [P, 2], F32)
        b_rz = sb("b_rz", [P, 2], F32)
        b_n = sb("b_n", [P, 2], F32)
        w_t = sb("w_t", [P, D], F32)
        w_max = sb("w_max", [P, 4], F32)
        diag_s = sb("diag_s", [P, D], F32)
        unscale = sb("unscale", [P, D], F32)
        w_s = sb("w_s", [D, D], F32)
        bias_b = sb("bias_b", [P, KT, D], F32)
        ident = sb("ident", [P, P], F32)
        ident2 = sb("ident2", [P, D], F32)
        tri = sb("tri", [P, P], BF16)
        ones = sb("ones", [P, P], BF16)
        code_bias = sb("code_bias", [P, 1], F32)

        bank = [ctx.enter_context(nc.psum_tensor(f"bank{i}", [P, CW], F32)) for i in range(4)]
        m_acc, rz_ps, n_ps, node_ps = bank
        wide = [ctx.enter_context(nc.psum_tensor(f"wide{i}", [P, PW], F32)) for i in range(2)]
        cnt = wide
        out_ps = [wide[0][:, 0:CW], wide[1][:, 0:CW]]

        x_loaded = sem("x_loaded")
        consts_loaded = sem("consts_loaded")
        adj_in = [sem(f"adj_in{i}") for i in range(SLOTS)]
        pair_used = sem("pair_used")
        mask_made = sem("mask_made")
        rsum_made = sem("rsum_made")
        cnt_done = sem("cnt_done")
        codes_made = sem("codes_made")
        xw_done = sem("xw_done")
        xw_copied = sem("xw_copied")
        high_copied = sem("high_copied")
        low_copied = sem("low_copied")
        m_ready = sem("m_ready")
        state_in = sem("state_in")
        gates_done = sem("gates_done")
        rz_made = sem("rz_made")
        t_made = sem("t_made")
        n_made = sem("n_made")
        d_made = sem("d_made")
        h_made = sem("h_made")
        h_stored = sem("h_stored")
        node_done = sem("node_done")
        s_mid_made = sem("s_mid_made")
        x_n_in = sem("x_n_in")
        y_made = sem("y_made")
        stats = sem("stats")
        var_made = sem("var_made")
        rstd_made = sem("rstd_made")
        x1_made = sem("x1_made")
        x1b_made = sem("x1b_made")
        x1t_done = sem("x1t_done")
        x1t_copied = sem("x1t_copied")
        sup_done = sem("sup_done")
        sup_high = sem("sup_high")
        sup_made = sem("sup_made")
        wexp_made = sem("wexp_made")
        block_done = sem("block_done")
        acc_zeroed = sem("acc_zeroed")
        acc_added = sem("acc_added")
        turned = sem("turned")
        o_made = sem("o_made")
        out_stored = [sem(f"out_stored{i}") for i in range(2)]
        set_pool = sem("set_pool")
        set_dve = sem("set_dve")
        scale_made = sem("scale_made")
        set_pe = sem("set_pe")
        w_s_made = sem("w_s_made")

        SET_POOL = 10

        block = ctx.enter_context(nc.Block())

        @block.sync
        def _(sp):
            def slot_free(freed, with_mask):
                sp.wait_ge(pair_used, freed)
                if with_mask:
                    sp.wait_ge(mask_made, freed)

            def load(q, src):
                sp.dma_start(stream[:, q % SLOTS, :], src).then_inc(adj_in[q % SLOTS], 16)

            def state(g, src):
                if g is not None:
                    sp.wait_ge(d_made, g)
                sp.dma_start(mx[D:P, :], src).then_inc(state_in, 16)

            def pass1(ic, first):
                for q in range(NP):
                    if not first or q >= SLOTS:
                        slot_free(ic * NP + q - SLOTS + 1, True)
                    if q == NP - 1:
                        state(None if first else 3 * ic - 2, x_t[:, bass.ts(ic, CW)])
                    load(q, adj_t[ic, NP - 1 - q])

            def pass2(ic, first):
                for q in range(NP):
                    slot_free((NCH + ic) * NP + q - SLOTS + 1, first and q < SLOTS)
                    if q == NP - 1:
                        sp.wait_ge(h_stored, 16 * (ic + 1))
                        state(3 * (NCH + ic) - 2, h_dram[:, bass.ts(ic, CW)])
                        if not first:
                            sp.wait_ge(y_made, ic)
                        sp.dma_start(x_n[:, :, :], x[ic]).then_inc(x_n_in, 16)
                    load(q, adj_t[ic, q])

            pass1(0, True)
            with sp.Fori(1, NCH) as ic:
                pass1(ic, False)
            pass2(0, True)
            with sp.Fori(1, NCH) as ic:
                pass2(ic, False)
            for b in range(NCH):
                sp.wait_ge(o_made, b + 1)
                sp.dma_start(out[b], o_n[:, b % 2, :, :]).then_inc(out_stored[b % 2], 16)
            for i in range(2):
                sp.wait_ge(out_stored[i], 16 * (NCH // 2))
            sp.wait_ge(h_stored, 16 * NCH)

        @block.tensor
        def _(pe):
            pe.wait_ge(x_loaded, 32)
            targets = [rz_ps[:, :], n_ps[:, :], node_ps[:, :], cnt[0][:, 0:CW], cnt[0][:, CW:PW],
                       cnt[1][:, 0:CW], cnt[1][:, CW:PW]]
            for u in range(NCH):
                c = NCH - 1 - u
                if u == 7:
                    pe.wait_ge(xw_copied, 1)
                for k in range(KT):
                    last = nc.tensor.matmul(targets[u % 7][:, k * D:(k + 1) * D],
                                            x_t_sb[:, (c * KT + k) * P:(c * KT + k + 1) * P],
                                            w12[0:D, :], start=True, stop=True)
                last.then_inc(xw_done, 1)

            def product(ic, q, pair, s, npass):
                if q % SLOTS == q:
                    pe.wait_ge(adj_in[q % SLOTS], 16 * ((ic + npass * NCH) * (NP // SLOTS) + 1))
                else:
                    pe.wait_ge(adj_in[q % SLOTS], 16 * ((ic + npass * NCH) * (NP // SLOTS) + 2))
                for u in range(2):
                    t = 2 * pair + u
                    last = nc.tensor.matmul(m_acc[D * u:D * (u + 1), :], s[:, t * D:(t + 1) * D],
                                            stream[:, q % SLOTS, u * CW:(u + 1) * CW],
                                            start=(q == 0), stop=(q == NP - 1))
                last.then_inc(pair_used, 1)

            def counts(ic, q, early):
                pe.wait_ge(mask_made, ic * NP + q + 1)
                if not early:
                    pe.wait_ge(codes_made, ic * NP + q - 1)
                r = q % RING
                m = [masks[:, r * PW + u * CW:r * PW + (u + 1) * CW] for u in range(2)]
                s = [rsums[:, r * PW + u * CW:r * PW + (u + 1) * CW] for u in range(2)]
                c = cnt[q % 2]
                nc.tensor.matmul(c[:, CW:PW], tri[:, :], m[1], start=True, stop=(q == 0))
                nc.tensor.matmul(c[:, 0:CW], tri[:, :], m[0], start=True, stop=False)
                if q == 0:
                    nc.tensor.matmul(c[:, 0:CW], ones[:, :], m[1], start=False, stop=True)\
                        .then_inc(cnt_done, 1)
                    return
                pe.wait_ge(rsum_made, ic * RSUMS + 2 * q)
                nc.tensor.matmul(c[:, CW:PW], ones[:, :], s[1], start=False, stop=True)
                nc.tensor.matmul(c[:, 0:CW], ones[:, :], s[0], start=False, stop=True)\
                    .then_inc(cnt_done, 1)

            def gates(g, layer, first):
                pe.wait_ge(m_ready, g + 1)
                pe.wait_ge(state_in, 16 * (g + 1))
                if not first:
                    pe.wait_ge(h_made, g)
                nc.tensor.matmul(rz_ps[:, :], w_rz[layer][:, :], mx[:, :], start=True, stop=True)
                nc.tensor.matmul(n_ps[:, :], w_n[layer][:, :], mx[:, :], start=True, stop=True)\
                    .then_inc(gates_done, 1)

            def node(g, layer, first, freed):
                pe.wait_ge(h_made, g + 1)
                if not first:
                    pe.wait_ge(*freed)
                rhs = (w12, ident2)[layer][D:P, :]
                for k in range(KT):
                    last = nc.tensor.matmul(node_ps[:, k * D:(k + 1) * D],
                                            h_c[D:P, k * P:(k + 1) * P], rhs, start=True, stop=True)
                last.then_inc(node_done, 1)

            def x1_turn(c):
                pe.wait_ge(x1_made, c + 1)
                for k in range(KT):
                    last = nc.tensor.matmul(node_ps[0:D, k * P:(k + 1) * P], x1[:, k, :],
                                            ident[:, :], start=True, stop=True)
                last.then_inc(x1t_done, 1)

            def support(c):
                pe.wait_ge(x1t_copied, c + 1)
                for k in range(KT):
                    last = nc.tensor.matmul(node_ps[:, k * D:(k + 1) * D],
                                            x1_t[:, k * P:(k + 1) * P], w_s[:, :],
                                            start=True, stop=True)
                last.then_inc(sup_done, 1)

            def product_block(c, b, early=False):
                if b == 0:
                    pe.wait_ge(sup_made, c + 1)
                pe.wait_ge(wexp_made, c * NCH + b + 1)
                if not early:
                    pe.wait_ge(acc_added, c * NCH + b - 1)
                for k in range(KT):
                    last = nc.tensor.matmul(out_ps[b % 2], sup[:, k, :, :],
                                            wexp[:, b % 2, k * CW:(k + 1) * CW],
                                            start=(k == 0), stop=(k == KT - 1))
                last.then_inc(block_done, 1)

            def m_acc_free(g):
                pe.wait_ge(high_copied, g)
                pe.wait_ge(low_copied, g)

            def pass1(ic, first, second=False):
                for q in range(NP):
                    if q > 0:
                        product(ic, q, NP - 1 - q, s_in, 0)
                        counts(ic, q - 1, first and q < 3)
                    elif first:
                        product(ic, q, NP - 1 - q, s_in, 0)
                    else:
                        counts(ic - 1, NP - 1, False)
                        m_acc_free(ic)
                        product(ic, q, NP - 1 - q, s_in, 0)
                    if not first:
                        if q == Q_GATES:
                            gates(ic - 1, 0, second)
                        if q == Q_NODE:
                            node(ic - 1, 0, second, (s_mid_made, ic - 1))

            pe.wait_ge(scale_made, 1)
            pe.wait_ge(xw_copied, 3)
            nc.tensor.matmul(node_ps[0:D, 0:D], w_t[0:D, :], diag_s[0:D, :], start=True, stop=True)\
                .then_inc(set_pe, 1)
            pe.wait_ge(xw_copied, NCH)
            pe.wait_ge(set_pool, SET_POOL)
            pass1(0, True)
            pe.wait_ge(w_s_made, 1)
            pass1(1, False, True)
            with pe.Fori(2, NCH) as ic:
                pass1(ic, False)

            def pass2(ic, deferred):
                for q in range(NP):
                    if q == 0:
                        if deferred == 0:
                            counts(NCH - 1, NP - 1, False)
                        m_acc_free(NCH + ic)
                    if deferred == 0 and q == 0:
                        pe.wait_ge(s_mid_made, NCH - 1)
                    if deferred == 0 and q == NP - KT // 2:
                        pe.wait_ge(s_mid_made, NCH)
                    product(ic, q, q, s_mid, 1)
                    if q == Q_GATES:
                        gates(NCH + ic - 1, 1 if deferred else 0, False)
                    if q == Q_NODE:
                        if deferred == 0:
                            node(NCH - 1, 0, False, (s_mid_made, NCH - 1))
                        else:
                            node(NCH + ic - 1, 1, deferred == 1, (sup_made, ic - 1))
                    if deferred:
                        if q == Q_X1T:
                            x1_turn(ic - 1)
                        if q == Q_SUP:
                            support(ic - 1)
                        if q in BLOCKS_LAG1:
                            product_block(ic - 1, BLOCKS_LAG1[q], deferred == 1 and BLOCKS_LAG1[q] < 2)
                    if deferred == 2 and q in BLOCKS_LAG2:
                        product_block(ic - 2, BLOCKS_LAG2[q])

            pass2(0, 0)
            pe.wait_ge(s_mid_made, NCH)
            pass2(1, 1)
            with pe.Fori(2, NCH) as ic:
                pass2(ic, 2)

            gates(2 * NCH - 1, 1, False)
            for b in sorted(BLOCKS_LAG2.values()):
                product_block(NCH - 2, b)
            node(2 * NCH - 1, 1, False, (sup_made, NCH - 1))
            x1_turn(NCH - 1)
            support(NCH - 1)

            def turn(b):
                pe.wait_ge(acc_added, (NCH - 1) * NCH + b + 1)
                if b >= 2:
                    pe.wait_ge(y_made, NCH + b - 1)
                for k in range(KT):
                    last = nc.tensor.matmul((rz_ps, n_ps)[b % 2][:, k * D:(k + 1) * D],
                                            out_acc[:, b * CW + k * P:b * CW + (k + 1) * P],
                                            unscale[:, :], start=True, stop=True)
                last.then_inc(turned, 1)

            for b in range(NCH):
                product_block(NCH - 1, b)
                if b > 0:
                    turn(b - 1)
            turn(NCH - 1)

        @block.scalar
        def _(act):
            act.dma_start(x_t_sb, x_t).then_inc(x_loaded, 16)
            act.dma_start(w12[0:D, :], w1).then_inc(x_loaded, 16)
            act.dma_start(w12[D:P, :], w2).then_inc(consts_loaded, 16)
            for half in range(2):
                act.dma_start(w_t[half * D:(half + 1) * D, :], weight_t).then_inc(consts_loaded, 16)
            act.wait_ge(set_pool, 2)
            for i, (wih, whh, bi, bh) in enumerate(((wih1_t, whh1_t, bih1, bhh1),
                                                    (wih2_t, whh2_t, bih2, bhh2))):
                act.dma_start(w_rz[i][0:D, :], wih[:, 0:P]).then_inc(consts_loaded, 16)
                act.dma_start(w_rz[i][D:P, :], whh[:, 0:P]).then_inc(consts_loaded, 16)
                act.dma_start(w_n[i][0:D, D:P], wih[:, P:3 * D]).then_inc(consts_loaded, 16)
                act.dma_start(w_n[i][D:P, 0:D], whh[:, P:3 * D]).then_inc(consts_loaded, 16)
                act.dma_start(b_i[:, i:i + 1], bi[0:P, :]).then_inc(consts_loaded, 16)
                act.dma_start(b_h[:, i:i + 1], bh[0:P, :]).then_inc(consts_loaded, 16)
                act.dma_start(b_n[0:D, i:i + 1], bh[P:3 * D, :]).then_inc(consts_loaded, 16)
                act.dma_start(b_n[D:P, i:i + 1], bi[P:3 * D, :]).then_inc(consts_loaded, 16)
            act.dma_start(bias_b[:, :, :], bias).then_inc(consts_loaded, 16)

            def code(ic, q):
                act.wait_ge(cnt_done, ic * NP + q + 1)
                at = (NP - 1 - q) * PW
                nc.scalar.activation(codes[:, bass.ds(ic * (NT * CW) + at, PW)], cnt[q % 2][:, :],
                                     ACT.Relu, bias=code_bias[:, :]).then_inc(codes_made, 1)

            def high(g, first):
                act.wait_ge(pair_used, (g + 1) * NP)
                if not first:
                    act.wait_ge(m_ready, g)
                nc.scalar.activation(m_high, m_acc[D:P, :], ACT.Copy).then_inc(high_copied, 1)

            def sigmoids(g, layer, first):
                act.wait_ge(gates_done, g + 1)
                if not first:
                    act.wait_ge(d_made, 3 * g)
                nc.scalar.activation(rz[:, :], rz_ps[:, :], ACT.Sigmoid,
                                     bias=b_rz[:, layer:layer + 1]).then_inc(rz_made, 1)

            def tanh(g, layer):
                act.wait_ge(t_made, 2 * (g + 1))
                nc.scalar.activation(n_g, t_n, ACT.Tanh,
                                     bias=b_n[D:P, layer:layer + 1]).then_inc(n_made, 1)

            def relu(g, first, stored=None, store_to=None):
                act.wait_ge(d_made, 3 * (g + 1))
                if not first:
                    act.wait_ge(node_done, g)
                if stored is not None:
                    act.wait_ge(h_stored, stored)
                nc.scalar.activation(h_c[D:P, :], t_n, ACT.Relu).then_inc(h_made, 1)
                if store_to is not None:
                    act.wait_ge(h_made, g + 1)
                    act.dma_start(store_to, h_c[D:P, :]).then_inc(h_stored, 16)

            def x1_turned(c):
                act.wait_ge(x1t_done, c + 1)
                nc.scalar.activation(x1_t, node_ps[0:D, :], ACT.Copy).then_inc(x1t_copied, 1)

            def split_high(c, first):
                act.wait_ge(sup_done, c + 1)
                if not first:
                    act.wait_ge(block_done, c * NCH)
                nc.scalar.activation(sup[:, :, 0, :],
                                     node_ps[:, 0:KT * D].rearrange("p (k d) -> p k d", d=D),
                                     ACT.Copy).then_inc(sup_high, 1)

            def expand(c, b, early=False):
                if not early:
                    act.wait_ge(block_done, c * NCH + b - 1)
                at = b * NT * CW
                nc.scalar.activation(wexp[:, b % 2, :].bitcast(U16),
                                     codes[:, bass.ds(c * (KT * CW) + at, KT * CW)], ACT.Copy,
                                     scale=float(P)).then_inc(wexp_made, 1)

            act.wait_ge(set_pool, SET_POOL)
            act.wait_ge(set_dve, 4)
            def pass1(ic, first, second=False):
                for q in range(NP):
                    if not first and q == 0:
                        high(ic - 1, second)
                        code(ic - 1, NP - 1)
                    if q > 0:
                        code(ic, q - 1)
                    if not first:
                        if q == Q_SIG:
                            sigmoids(ic - 1, 0, second)
                        if q == Q_TANH:
                            tanh(ic - 1, 0)
                        if q == Q_RELU:
                            relu(ic - 1, second, None if second else 16 * (ic - 1),
                                 h_dram[:, bass.ts(ic - 1, CW)])

            pass1(0, True)
            pass1(1, False, True)
            with act.Fori(2, NCH) as ic:
                pass1(ic, False)

            def pass2(ic, deferred):
                g = NCH + ic - 1
                layer = 1 if deferred else 0
                ahead1 = {q - 1: b for q, b in BLOCKS_LAG1.items()}
                ahead2 = {q - 1: b for q, b in BLOCKS_LAG2.items() if q}
                for q in range(NP):
                    if q == 0:
                        high(g, False)
                        if deferred == 0:
                            code(NCH - 1, NP - 1)
                        if deferred == 2:
                            expand(ic - 2, BLOCKS_LAG2[0])
                    if q == Q_SIG:
                        sigmoids(g, layer, False)
                    if q == Q_TANH:
                        tanh(g, layer)
                    if q == Q_RELU:
                        if deferred == 0:
                            relu(g, False, 16 * (NCH - 1), h_dram[:, bass.ts(NCH - 1, CW)])
                        else:
                            relu(g, False, 16 * NCH if deferred == 1 else None)
                    if deferred:
                        if q == Q_X1T:
                            x1_turned(ic - 1)
                        if q == Q_SPLIT:
                            split_high(ic - 1, deferred == 1)
                        if q in ahead1:
                            expand(ic - 1, ahead1[q], deferred == 1 and ahead1[q] < 2)
                    if deferred == 2 and q in ahead2:
                        expand(ic - 2, ahead2[q])

            pass2(0, 0)
            pass2(1, 1)
            with act.Fori(2, NCH) as ic:
                pass2(ic, 2)
            g = 2 * NCH - 1
            high(g, False)
            expand(NCH - 2, 4)
            sigmoids(g, 1, False)
            expand(NCH - 2, 5)
            tanh(g, 1)
            expand(NCH - 2, 6)
            relu(g, False)
            expand(NCH - 2, 7)
            x1_turned(NCH - 1)
            split_high(NCH - 1, False)
            for b in range(NCH):
                expand(NCH - 1, b)

        @block.gpsimd
        def _(pool):
            for i in range(2):
                nc.gpsimd.memset(w_n[i][:, :], 0.0).then_inc(set_pool, 1)
            nc.gpsimd.memset(ident[:, :], 0.0).then_inc(set_pool, 1)
            nc.gpsimd.memset(tri[:, :], -1.0).then_inc(set_pool, 1)
            nc.gpsimd.memset(ones[:, :], -1.0).then_inc(set_pool, 1)
            nc.gpsimd.memset(code_bias[:, :], float(NEIGH - BIG)).then_inc(set_pool, 1)
            nc.gpsimd.memset(mhalf[:, :], -0.5).then_inc(set_pool, 1)
            pool.wait_ge(set_pool, 7)
            nc.gpsimd.affine_select(out=ident[:, :], in_=ident[:, :], compare_op=ALU.not_equal,
                                    fill=1.0, base=0, pattern=[[-1, P]],
                                    channel_multiplier=1).then_inc(set_pool, 1)
            nc.gpsimd.affine_select(out=tri[:, :], in_=tri[:, :], compare_op=ALU.is_gt, fill=0.0,
                                    base=0, pattern=[[-1, P]], channel_multiplier=1)\
                .then_inc(set_pool, 1)
            pool.wait_ge(set_pool, 9)
            nc.gpsimd.affine_select(out=tri[:, :], in_=tri[:, :], compare_op=ALU.not_equal,
                                    fill=float(BIG), base=0, pattern=[[-1, P]],
                                    channel_multiplier=1).then_inc(set_pool, SET_POOL - 9)
            pool.wait_ge(cnt_done, NCH * NP)
            pool.wait_ge(rsum_made, NCH * RSUMS)
            nc.gpsimd.memset(out_acc, 0.0).then_inc(acc_zeroed, 1)

            def rstd(c):
                pool.wait_ge(var_made, c + 1)
                nc.gpsimd.tensor_tensor(stat[:, 4, :], stat[:, 3, :], mhalf[:, :], ALU.pow)\
                    .then_inc(rstd_made, 1)

            def add_bias(c):
                pool.wait_ge(x1_made, c + 1)
                nc.gpsimd.tensor_tensor(
                    x1b[:, bass.ts(c, KT * D)].rearrange("p (k d) -> p k d", d=D),
                    x1[:, :, :], bias_b[:, :, :], ALU.add).then_inc(x1b_made, 1)

            pool.wait_ge(pair_used, NCH * NP)
            with pool.Fori(0, NCH) as c:
                rstd(c)
                add_bias(c)
            for b in range(NCH):
                rstd(NCH + b)

        @block.vector
        def _(dve):
            def xw_copy(u):
                c = NCH - 1 - u
                dve.wait_ge(xw_done, u + 1)
                src = [rz_ps[:, 0:KT * D], n_ps[:, 0:KT * D], node_ps[:, 0:KT * D],
                       cnt[0][:, 0:KT * D], cnt[0][:, CW:CW + KT * D],
                       cnt[1][:, 0:KT * D], cnt[1][:, CW:CW + KT * D]][u % 7]
                nc.vector.tensor_copy(s_in[:, c * KT * D:(c + 1) * KT * D], src)\
                    .then_inc(xw_copied, 1)

            for u in range(NCH):
                xw_copy(u)
            dve.wait_ge(consts_loaded, 16 * 20)
            nc.vector.tensor_reduce(w_max[:, 0:1], w_t[:, :], AX_X, ALU.max,
                                    apply_absolute_value=True).then_inc(set_dve, 1)
            dve.wait_ge(set_dve, 1)
            nc.vector.tensor_scalar(w_max[:, 1:2], w_max[:, 0:1], 2.0 ** -100, None, ALU.max)\
                .then_inc(set_dve, 1)
            dve.wait_ge(set_dve, 2)
            nc.vector.tensor_scalar(w_max[:, 2:3].bitcast(I32), w_max[:, 1:2].bitcast(I32),
                                    0x7F800000, None, ALU.bitwise_and).then_inc(set_dve, 1)
            nc.vector.tensor_tensor(b_rz[:, :], b_i[:, :], b_h[:, :], ALU.add).then_inc(set_dve, 1)
            dve.wait_ge(set_dve, 3)
            nc.vector.tensor_scalar(w_max[:, 3:4].bitcast(I32), w_max[:, 2:3].bitcast(I32), -1.0,
                                    254.0 * EXP_ONE, ALU.mult, ALU.add).then_inc(set_dve, 1)
            dve.wait_ge(set_pool, SET_POOL)
            nc.vector.tensor_copy(ident2[0:D, :], ident[0:D, 0:D]).then_inc(set_dve, 1)
            nc.vector.tensor_copy(ident2[D:P, :], ident[D:P, D:P]).then_inc(set_dve, 1)
            dve.wait_ge(set_dve, 7)
            nc.vector.tensor_scalar(diag_s[:, :], ident2[:, :], w_max[:, 3:4], 2.0 ** 8,
                                    ALU.mult, ALU.mult).then_inc(scale_made, 1)
            nc.vector.tensor_scalar(unscale[:, :], ident2[:, :], w_max[:, 2:3],
                                    2.0 ** (CODE_SHIFT - 8), ALU.mult, ALU.mult).then_inc(set_dve, 1)

            def mask_and_sums(ic, q, early):
                r, g = q % RING, ic * NP + q
                if q < SLOTS:
                    dve.wait_ge(adj_in[q], 16 * (ic * (NP // SLOTS) + 1))
                else:
                    dve.wait_ge(adj_in[q - SLOTS], 16 * (ic * (NP // SLOTS) + 2))
                if not early:
                    dve.wait_ge(cnt_done, g - RING + 1)
                nc.vector.tensor_scalar(masks[:, r * PW:(r + 1) * PW], stream[:, q % SLOTS, :],
                                        0.0, None, ALU.not_equal).then_inc(mask_made, 1)
                if q == 0:
                    return
                b = (q - 1) % RING
                m_before = [masks[:, b * PW + u * CW:b * PW + (u + 1) * CW] for u in range(2)]
                s_before = rsums[:, b * PW:b * PW + CW] if q > 1 else m_before[1]
                s = [rsums[:, r * PW + u * CW:r * PW + (u + 1) * CW] for u in range(2)]
                if q > 1:
                    dve.wait_ge(rsum_made, ic * RSUMS + 2 * (q - 1))
                else:
                    dve.wait_ge(mask_made, g)
                nc.vector.tensor_tensor(s[1], s_before, m_before[0], ALU.add).then_inc(rsum_made, 1)
                dve.wait_ge(rsum_made, ic * RSUMS + 2 * q - 1)
                dve.wait_ge(mask_made, g + 1)
                nc.vector.tensor_tensor(s[0], s[1], masks[:, r * PW + CW:(r + 1) * PW], ALU.add)\
                    .then_inc(rsum_made, 1)

            def low(g, first):
                dve.wait_ge(pair_used, (g + 1) * NP)
                if not first:
                    dve.wait_ge(gates_done, g)
                nc.vector.tensor_copy(mx[0:D, :], m_acc[0:D, :]).then_inc(low_copied, 1)

            def add_halves(g):
                dve.wait_ge(low_copied, g + 1)
                dve.wait_ge(high_copied, g + 1)
                nc.vector.tensor_tensor(mx[0:D, :], mx[0:D, :], m_high, ALU.add)\
                    .then_inc(m_ready, 1)

            def n_input(g, layer, first):
                dve.wait_ge(rz_made, g + 1)
                if not first:
                    dve.wait_ge(h_made, g)
                nc.vector.scalar_tensor_tensor(t_n, n_ps[0:D, :], b_n[0:D, layer:layer + 1],
                                               rz[0:D, :], ALU.add, ALU.mult).then_inc(t_made, 1)
                dve.wait_ge(t_made, 2 * g + 1)
                nc.vector.tensor_tensor(t_n, t_n, n_ps[D:P, :], ALU.add)\
                    .then_inc(t_made, 1)

            def new_h(g):
                dve.wait_ge(n_made, g + 1)
                nc.vector.tensor_tensor(t_n, mx[D:P, :], n_g, ALU.subtract)\
                    .then_inc(d_made, 1)
                dve.wait_ge(d_made, 3 * g + 1)
                nc.vector.tensor_tensor(t_n, t_n, rz[D:P, :], ALU.mult)\
                    .then_inc(d_made, 1)
                dve.wait_ge(d_made, 3 * g + 2)
                nc.vector.tensor_tensor(t_n, t_n, n_g, ALU.add)\
                    .then_inc(d_made, 1)

            def to_s_mid(c):
                dve.wait_ge(node_done, c + 1)
                nc.vector.tensor_copy(s_mid[:, bass.ts(c, KT * D)], node_ps[:, 0:KT * D])\
                    .then_inc(s_mid_made, 1)

            def pass1(ic, first, second=False):
                for q in range(NP):
                    if not first and q == 0:
                        low(ic - 1, second)
                    mask_and_sums(ic, q, first and q < RING)
                    if not first:
                        if q == 0:
                            add_halves(ic - 1)
                        if q == Q_T:
                            n_input(ic - 1, 0, second)
                        if q == Q_H:
                            new_h(ic - 1)
                        if q == Q_NODE_OUT:
                            to_s_mid(ic - 1)

            dve.wait_ge(set_pe, 1)
            nc.vector.tensor_copy(w_s[:, :], node_ps[0:D, 0:D]).then_inc(w_s_made, 1)
            pass1(0, True)
            pass1(1, False, True)
            with dve.Fori(2, NCH) as ic:
                pass1(ic, False)

            def norm(n, into, free):
                nc.vector.tensor_reduce(stat[:, 0, :], y[:, :, :], AX_X, ALU.add).then_inc(stats, 1)
                dve.wait_ge(stats, 5 * n + 1)
                nc.vector.tensor_scalar(stat[:, 1, :], stat[:, 0, :], -1.0 / D, None, ALU.mult)\
                    .then_inc(stats, 1)
                dve.wait_ge(stats, 5 * n + 2)
                nc.vector.tensor_tensor(y[:, :, :], y[:, :, :],
                                        stat[:, 1, :].unsqueeze(2).to_broadcast([P, KT, D]),
                                        ALU.add).then_inc(stats, 1)
                dve.wait_ge(stats, 5 * n + 3)
                nc.vector.tensor_tensor(sq[:, :, :], y[:, :, :], y[:, :, :], ALU.mult)\
                    .then_inc(stats, 1)
                dve.wait_ge(stats, 5 * n + 4)
                nc.vector.tensor_reduce(stat[:, 2, :], sq[:, :, :], AX_X, ALU.add).then_inc(stats, 1)
                dve.wait_ge(stats, 5 * n + 5)
                nc.vector.tensor_scalar(stat[:, 3, :], stat[:, 2, :], 1.0 / D, EPS,
                                        ALU.mult, ALU.add).then_inc(var_made, 1)
                dve.wait_ge(rstd_made, n + 1)
                if free is not None:
                    dve.wait_ge(*free)
                return nc.vector.tensor_tensor(into, y[:, :, :],
                                               stat[:, 4, :].unsqueeze(2).to_broadcast([P, KT, D]),
                                               ALU.mult)

            def norm1(c, first):
                dve.wait_ge(node_done, NCH + c + 1)
                dve.wait_ge(x_n_in, 16 * (c + 1))
                nc.vector.tensor_tensor(y[:, :, :],
                                        node_ps[:, 0:KT * D].rearrange("p (k d) -> p k d", d=D),
                                        x_n[:, :, :], ALU.add).then_inc(y_made, 1)
                dve.wait_ge(y_made, c + 1)
                if not first:
                    dve.wait_ge(x1t_done, c)
                norm(c, x1[:, :, :], None if first else (x1b_made, c)).then_inc(x1_made, 1)

            def split_low(c):
                dve.wait_ge(sup_high, c + 1)
                nc.vector.tensor_tensor(sup[:, :, 1, :],
                                        node_ps[:, 0:KT * D].rearrange("p (k d) -> p k d", d=D),
                                        sup[:, :, 0, :], ALU.subtract).then_inc(sup_made, 1)

            def accumulate(c, b):
                dve.wait_ge(block_done, c * NCH + b + 1)
                at = out_acc[:, b * CW:(b + 1) * CW]
                nc.vector.tensor_tensor(at, out_ps[b % 2], at, ALU.add).then_inc(acc_added, 1)

            def pass2(ic, deferred):
                g = NCH + ic - 1
                layer = 1 if deferred else 0
                for q in range(NP):
                    if q == 0:
                        low(g, False)
                        add_halves(g)
                    if q == Q_T:
                        n_input(g, layer, False)
                    if q == Q_H:
                        new_h(g)
                    if q == Q_NODE_OUT:
                        if deferred:
                            norm1(ic - 1, deferred == 1)
                        else:
                            to_s_mid(NCH - 1)
                    if deferred and q == Q_SPLIT:
                        split_low(ic - 1)
                    if deferred == 2 and q in BLOCKS_LAG2:
                        accumulate(ic - 2, BLOCKS_LAG2[q])
                    if deferred and q in BLOCKS_LAG1:
                        if deferred == 1 and BLOCKS_LAG1[q] == 0:
                            dve.wait_ge(acc_zeroed, 1)
                        accumulate(ic - 1, BLOCKS_LAG1[q])

            pass2(0, 0)
            pass2(1, 1)
            with dve.Fori(2, NCH) as ic:
                pass2(ic, 2)
            g = 2 * NCH - 1
            low(g, False)
            add_halves(g)
            accumulate(NCH - 2, 4)
            n_input(g, 1, False)
            accumulate(NCH - 2, 5)
            new_h(g)
            accumulate(NCH - 2, 6)
            accumulate(NCH - 2, 7)
            norm1(NCH - 1, False)
            split_low(NCH - 1)

            def finish(b):
                dve.wait_ge(turned, b + 1)
                dve.wait_ge(x1b_made, NCH)
                if b > 0:
                    dve.wait_ge(o_made, b)
                nc.vector.tensor_tensor(
                    y[:, :, :], (rz_ps, n_ps)[b % 2][:, 0:KT * D].rearrange("p (k d) -> p k d", d=D),
                    x1b[:, b * KT * D:(b + 1) * KT * D].rearrange("p (k d) -> p k d", d=D),
                    ALU.add).then_inc(y_made, 1)
                dve.wait_ge(y_made, NCH + b + 1)
                norm(NCH + b, o_n[:, b % 2, :, :], None if b < 2 else (out_stored[b % 2], 16 * (b // 2)))\
                    .then_inc(o_made, 1)

            for b in range(NCH):
                accumulate(NCH - 1, b)
                if b > 0:
                    finish(b - 1)
            finish(NCH - 1)


def kernel(x, adj, L0_gnn_W1, L0_gnn_wih1, L0_gnn_whh1, L0_gnn_bih1, L0_gnn_bhh1, L0_gnn_W2,
           L0_gnn_wih2, L0_gnn_whh2, L0_gnn_bih2, L0_gnn_bhh2, L1_gnn_weight, L1_gnn_bias):
    import numpy as np
    import concourse.bacc as bacc
    from concourse.bass_utils import run_bass_kernel_spmd

    adj_t = np.ascontiguousarray(
        np.asarray(adj).reshape(NCH, CW, NP, 2, P).transpose(0, 2, 4, 3, 1)).reshape(NCH, NP, P, PW)
    arrays = {
        "adj_t": adj_t,
        "x_t": np.ascontiguousarray(np.asarray(x).T),
        "x": np.ascontiguousarray(x),
        "w1": np.ascontiguousarray(L0_gnn_W1),
        "w2": np.ascontiguousarray(L0_gnn_W2),
        "wih1_t": np.ascontiguousarray(np.asarray(L0_gnn_wih1).T),
        "whh1_t": np.ascontiguousarray(np.asarray(L0_gnn_whh1).T),
        "wih2_t": np.ascontiguousarray(np.asarray(L0_gnn_wih2).T),
        "whh2_t": np.ascontiguousarray(np.asarray(L0_gnn_whh2).T),
        "bih1": np.ascontiguousarray(L0_gnn_bih1).reshape(3 * D, 1),
        "bhh1": np.ascontiguousarray(L0_gnn_bhh1).reshape(3 * D, 1),
        "bih2": np.ascontiguousarray(L0_gnn_bih2).reshape(3 * D, 1),
        "bhh2": np.ascontiguousarray(L0_gnn_bhh2).reshape(3 * D, 1),
        "weight_t": np.ascontiguousarray(np.asarray(L1_gnn_weight).T),
        "bias": np.ascontiguousarray(L1_gnn_bias).reshape(1, D),
    }
    nc = bacc.Bacc("TRN2", target_bir_lowering=False, num_devices=1, dynamic_dma_scratch_size=1024)
    aps = {name: nc.dram_tensor(f"in_{name}", a.shape, mybir.dt.from_np(a.dtype),
                                kind="ExternalInput").ap() for name, a in arrays.items()}
    out = nc.dram_tensor("out_nodes", (N, D), F32, kind="ExternalOutput").ap()
    h_dram = nc.dram_tensor("h_dram", (D, N), F32, kind="Internal").ap()
    aps["x"] = aps["x"].rearrange("(c k p) d -> c p k d", k=KT, p=P)
    aps["bias"] = aps["bias"].unsqueeze(1).to_broadcast([P, KT, D])
    build(nc, out=out.rearrange("(c k p) d -> c p k d", k=KT, p=P), h_dram=h_dram, **aps)
    r = run_bass_kernel_spmd(nc, [{f"in_{name}": a for name, a in arrays.items()}], core_ids=[0])
    return r.results[0]["out_nodes"]
```

```python
from contextlib import ExitStack

import concourse.bass as bass
from concourse import mybir

F32 = mybir.dt.float32
BF16 = mybir.dt.bfloat16
F16 = mybir.dt.float16
U8 = mybir.dt.uint8
U16 = mybir.dt.uint16
I32 = mybir.dt.int32
ALU = mybir.AluOpType
ACT = mybir.ActivationFunctionType
AX_X = mybir.AxisListType.X

P = 128
N = 4096
D = 64
CW = 512
NCH = N // CW
KT = CW // P
NT = N // P
NP = NT // 2
NQ = NT // 4
PW = 2 * CW
QW = 4 * CW
SLOTS = 8
NEIGH = 100
BIG = 128
CODE_SHIFT = 27
EXP_ONE = 1 << 23
EPS = 1e-5
RSUMS = NT - 2
SET_POOL = 12
ACC_READY = 4

P1_GATES, P1_SIG, P1_T, P1_TANH, P1_H, P1_RELU, P1_NODE, P1_OUT = 0, 1, 2, 3, 4, 5, 5, 6
P2_GATES, P2_SIG, P2_T, P2_TANH, P2_H, P2_RELU, P2_NODE = 1, 2, 3, 4, 5, 6, 7
P2_SQUARE, P2_NORM, P2_X1T, P2_SUP, P2_SPLIT, P2_CENTER = 8, 9, 11, 12, 14, 15
BLOCKS = {0: 0, 2: 1, 4: 2, 6: 3, 8: 4, 10: 5, 12: 6, 13: 7}


def build(nc, adj_t, x_t, w1, w2, wih1_t, whh1_t, wih2_t, whh2_t, bih1, bhh1, bih2, bhh2,
          weight_t, bias, out, h_dram):
    with ExitStack() as ctx:
        def sb(name, shape, dt):
            return ctx.enter_context(nc.sbuf_tensor(name, shape, dt))

        def sem(name):
            return ctx.enter_context(nc.semaphore(name))

        codes = sb("codes", [P, NCH * NT * CW], U8)
        x_t_sb = codes[0:D, (NCH - 1) * NT * CW:].bitcast(F32)
        stream = sb("stream", [P, SLOTS, PW], F32)
        last_w = stream[:, :, :].bitcast(BF16)
        s_in = sb("s_in", [P, NT * D], F32)
        x1b = s_in
        s_mid = sb("s_mid", [P, NT * D], F32)
        end = s_mid[:, :].rearrange("p (r k d) -> p r k d", k=KT, d=D)
        y, ysq, o_n = end[:, 0:4], end[:, 4:6], end[:, 6:8]
        shared = sb("shared", [P, NCH * CW], F32)
        out_acc = shared[:, :]
        masks = shared[:, 0:QW].bitcast(BF16)
        rsums = shared[:, QW:2 * QW].bitcast(BF16)
        wexp = sb("wexp", [P, 2, KT * CW], BF16)
        mx = sb("mx", [P, CW], F32)
        m_high_t = sb("m_high_t", [P, CW], F32)
        m_high = m_high_t[0:D, :]
        t_n = m_high_t[D:P, :]
        rz = sb("rz", [P, CW], F32)
        x1_t_n = sb("x1_t_n", [P, CW], F32)
        x1_t = x1_t_n[0:D, :]
        n_g = x1_t_n[D:P, :]
        h_c = sb("h_c", [P, CW], F32)
        sq = sb("sq", [P, KT, D], F32)
        x1 = sb("x1", [P, KT, D], F32)
        xb = sb("xb", [P, KT, D], F32)
        stat = sb("stat", [P, 4, KT], F32)
        var = sb("var", [P, 4, KT], F32)
        rstd = sb("rstd", [P, 4, KT], F32)
        mhalf = sb("mhalf", [P, KT], F32)
        sup = sb("sup", [P, KT, 2, D], F16)
        w_rz = [sb(f"w_rz{i}", [P, P], F32) for i in range(2)]
        w_n = [sb(f"w_n{i}", [P, P], F32) for i in range(2)]
        w12 = sb("w12", [P, D], F32)
        b_i = sb("b_i", [P, 2], F32)
        b_h = sb("b_h", [P, 2], F32)
        b_rz = sb("b_rz", [P, 2], F32)
        b_n = sb("b_n", [P, 2], F32)
        w_t = sb("w_t", [P, D], F32)
        w_max = sb("w_max", [P, 4], F32)
        diag_s = sb("diag_s", [P, D], F32)
        unscale = sb("unscale", [P, D], F32)
        w_s = sb("w_s", [D, D], F32)
        bias_b = sb("bias_b", [P, KT, D], F32)
        ident = sb("ident", [P, P], F32)
        ident2 = sb("ident2", [P, D], F32)
        centre = sb("centre", [P, D], F32)
        tri = sb("tri", [P, P], BF16)
        neg_ones = sb("neg_ones", [P, P], BF16)
        code_bias = sb("code_bias", [P, 1], F32)

        m_acc, rz_ps, n_ps, spare_ps = [
            ctx.enter_context(nc.psum_tensor(f"bank{i}", [P, CW], F32)) for i in range(4)]
        node_ps = rz_ps
        cnt = [ctx.enter_context(nc.psum_tensor(f"wide{i}", [P, PW], F32)) for i in range(2)]
        out_ps = [cnt[0][:, 0:CW], cnt[1][:, 0:CW], cnt[0][:, CW:PW], cnt[1][:, CW:PW]]
        turn_ps = [n_ps, spare_ps, m_acc, rz_ps]

        def nodes(ps):
            return ps[:, 0:KT * D].rearrange("p (k d) -> p k d", d=D)

        x_first, x_rest, consts_loaded = sem("x_first"), sem("x_rest"), sem("consts_loaded")
        adj_in = [sem(f"adj_in{i}") for i in range(SLOTS)]
        pair_used, mask_made, rsum_made = sem("pair_used"), sem("mask_made"), sem("rsum_made")
        cnt_done, codes_made = sem("cnt_done"), sem("codes_made")
        xw_done, xw_copied = sem("xw_done"), sem("xw_copied")
        high_copied, low_copied, m_ready = sem("high_copied"), sem("low_copied"), sem("m_ready")
        state_in, gates_done, rz_made = sem("state_in"), sem("gates_done"), sem("rz_made")
        t_made, n_made, d_made, h_made = sem("t_made"), sem("n_made"), sem("d_made"), sem("h_made")
        h_stored, node_done, s_mid_made = sem("h_stored"), sem("node_done"), sem("s_mid_made")
        x_c_in, sq_made, sums_of_sq = sem("x_c_in"), sem("sq_made"), sem("sums_of_sq")
        var_made, rstd_made, x1_made = sem("var_made"), sem("rstd_made"), sem("x1_made")
        xb_made, centred, x1b_made = sem("xb_made"), sem("centred"), sem("x1b_made")
        x1t_done, x1t_copied = sem("x1t_done"), sem("x1t_copied")
        sup_done, sup_high, sup_made = sem("sup_done"), sem("sup_high"), sem("sup_made")
        wexp_made = [sem(f"wexp_made{i}") for i in range(2)]
        last_w_made = [sem(f"last_w_made{i}") for i in range(2)]
        block_done, acc_added = sem("block_done"), sem("acc_added")
        turned, y_made, o_made = sem("turned"), sem("y_made"), sem("o_made")
        out_stored = [sem(f"out_stored{i}") for i in range(2)]
        set_pool, set_dve, scale_made = sem("set_pool"), sem("set_dve"), sem("scale_made")
        set_pe, w_s_made = sem("set_pe"), sem("w_s_made")

        block = ctx.enter_context(nc.Block())

        @block.sync
        def _(sp):
            def slot_free(freed, with_mask):
                sp.wait_ge(pair_used, freed)
                if with_mask:
                    sp.wait_ge(mask_made, freed)

            def load(q, src):
                sp.dma_start(stream[:, q % SLOTS, :], src).then_inc(adj_in[q % SLOTS], 16)

            def state(g, src):
                if g is not None:
                    sp.wait_ge(d_made, g)
                sp.dma_start(mx[D:P, :], src).then_inc(state_in, 16)

            def pass1(ic, first):
                for q in range(NP):
                    if not first or q >= SLOTS:
                        slot_free(ic * NP + q - SLOTS + 1, True)
                    if q == NP - 1:
                        state(None if first else 3 * ic - 2, x_t[:, bass.ts(ic, CW)])
                    load(q, adj_t[ic, NP - 1 - q])
                    if first and q == 1:
                        sp.dma_start(x_t_sb[:, 0:N - CW], x_t[:, 0:N - CW]).then_inc(x_rest, 16)

            def pass2(ic, first):
                for q in range(NP):
                    slot_free((NCH + ic) * NP + q - SLOTS + 1, first and q < SLOTS)
                    if q == NP - 1:
                        sp.wait_ge(h_stored, 16 * (ic + 1))
                        state(3 * (NCH + ic) - 2, h_dram[:, bass.ts(ic, CW)])
                        if not first:
                            sp.wait_ge(node_done, NCH + ic)
                        sp.dma_start(h_c[0:D, :], x_t[:, bass.ts(ic, CW)]).then_inc(x_c_in, 16)
                    load(q, adj_t[ic, q])

            sp.dma_start(x_t_sb[:, N - CW:N], x_t[:, N - CW:N]).then_inc(x_first, 16)
            sp.dma_start(w12[0:D, :], w1).then_inc(x_first, 16)
            pass1(0, True)
            with sp.Fori(1, NCH) as ic:
                pass1(ic, False)
            pass2(0, True)
            with sp.Fori(1, NCH) as ic:
                pass2(ic, False)
            for b in range(NCH):
                sp.wait_ge(o_made, b + 1)
                sp.dma_start(out[b], o_n[:, b % 2]).then_inc(out_stored[b % 2], 16)
            for i in range(2):
                sp.wait_ge(out_stored[i], 16 * (NCH // 2))
            sp.wait_ge(h_stored, 16 * NCH)

        @block.tensor
        def _(pe):
            def x_w1(u):
                if u == 0:
                    pe.wait_ge(x_first, 32)
                if u == 1:
                    pe.wait_ge(x_rest, 16)
                if u >= 2:
                    pe.wait_ge(xw_copied, u - 1)
                c = NCH - 1 - u
                for k in range(KT):
                    last = nc.tensor.matmul((rz_ps, n_ps)[u % 2][:, k * D:(k + 1) * D],
                                            x_t_sb[:, (c * KT + k) * P:(c * KT + k + 1) * P],
                                            w12[0:D, :], start=True, stop=True)
                last.then_inc(xw_done, 1)

            def product(ic, q, pair, s, npass):
                pe.wait_ge(adj_in[q % SLOTS],
                           16 * ((ic + npass * NCH) * (NP // SLOTS) + q // SLOTS + 1))
                for u in range(2):
                    t = 2 * pair + u
                    last = nc.tensor.matmul(m_acc[D * u:D * (u + 1), :], s[:, t * D:(t + 1) * D],
                                            stream[:, q % SLOTS, u * CW:(u + 1) * CW],
                                            start=(q == 0), stop=(q == NP - 1))
                last.then_inc(pair_used, 1)

            def counts(ic, qd, early):
                r = qd % 2
                pe.wait_ge(mask_made, ic * NP + 2 * qd + 2)
                m = [masks[:, r * QW + u * CW:r * QW + (u + 1) * CW] for u in range(4)]
                s = [rsums[:, r * QW + u * CW:r * QW + (u + 1) * CW] for u in range(4)]
                if qd == 0:
                    s[3], s[2] = None, m[3]
                pe.wait_ge(rsum_made, ic * RSUMS + (4 * qd + 2))
                for u in (3, 2, 1, 0):
                    if not early and u % 2:
                        pe.wait_ge(codes_made, 2 * (ic * NQ + qd) - (1 if u == 3 else 0))
                    to = cnt[u // 2][:, (u % 2) * CW:(u % 2 + 1) * CW]
                    last = nc.tensor.matmul(to, tri[:, :], m[u], start=True, stop=s[u] is None)
                    if s[u] is not None:
                        last = nc.tensor.matmul(to, neg_ones[:, :], s[u], start=False, stop=True)
                last.then_inc(cnt_done, 1)

            def gates(g, layer, free):
                pe.wait_ge(m_ready, g + 1)
                pe.wait_ge(state_in, 16 * (g + 1))
                for f in free:
                    pe.wait_ge(*f)
                nc.tensor.matmul(rz_ps[:, :], w_rz[layer][:, :], mx[:, :], start=True, stop=True)
                nc.tensor.matmul(n_ps[:, :], w_n[layer][:, :], mx[:, :], start=True, stop=True)\
                    .then_inc(gates_done, 1)

            def node(g, layer):
                pe.wait_ge(h_made, g + 1)
                if layer:
                    pe.wait_ge(x_c_in, 16 * (g - NCH + 1))
                lo, rhs = (D, w12) if layer == 0 else (0, centre)
                for k in range(KT):
                    last = nc.tensor.matmul(node_ps[:, k * D:(k + 1) * D],
                                            h_c[lo:P, k * P:(k + 1) * P], rhs[lo:P, :],
                                            start=True, stop=True)
                last.then_inc(node_done, 1)

            def x1_turn(c):
                pe.wait_ge(x1_made, c + 1)
                for k in range(KT):
                    last = nc.tensor.matmul(node_ps[0:D, k * P:(k + 1) * P], x1[:, k, :],
                                            ident[:, :], start=True, stop=True)
                last.then_inc(x1t_done, 1)

            def support(c):
                pe.wait_ge(x1t_copied, c + 1)
                for k in range(KT):
                    last = nc.tensor.matmul(node_ps[:, k * D:(k + 1) * D],
                                            x1_t[:, k * P:(k + 1) * P], w_s[:, :],
                                            start=True, stop=True)
                last.then_inc(sup_done, 1)

            def product_block(c, b, early=False, at_end=False):
                if b == 0:
                    pe.wait_ge(sup_made, c + 1)
                if at_end:
                    pe.wait_ge(last_w_made[b % 2], b // 2 + 1)
                    w = last_w[:, b, :]
                else:
                    pe.wait_ge(wexp_made[b % 2], c * (NCH // 2) + b // 2 + 1)
                    w = wexp[:, b % 2, :]
                if not early:
                    pe.wait_ge(acc_added, c * NCH + b - 3 + ACC_READY)
                for k in range(KT):
                    last = nc.tensor.matmul(out_ps[b % 4], sup[:, k, :, :],
                                            w[:, k * CW:(k + 1) * CW],
                                            start=(k == 0), stop=(k == KT - 1))
                last.then_inc(block_done, 1)

            def m_acc_free(g):
                pe.wait_ge(high_copied, g)
                pe.wait_ge(low_copied, g)

            def pass1(ic, first, second=False):
                for qd in range(NQ):
                    if qd == 0 and not first:
                        m_acc_free(ic)
                    if first:
                        pe.wait_ge(xw_copied, qd + 1)
                    for q in (2 * qd, 2 * qd + 1):
                        product(ic, q, NP - 1 - q, s_in, 0)
                    if first and qd < NQ - 1:
                        x_w1(qd + 1)
                    if qd > 0:
                        counts(ic, qd - 1, first and qd == 1)
                    elif not first:
                        counts(ic - 1, NQ - 1, False)
                    if not first:
                        if qd == P1_GATES:
                            gates(ic - 1, 0, [(w_s_made, 1)] if second else
                                  [(h_made, ic - 1), (s_mid_made, ic - 1)])
                        if qd == P1_NODE:
                            node(ic - 1, 0)

            x_w1(0)
            pe.wait_ge(set_pool, SET_POOL)
            pass1(0, True)
            pe.wait_ge(scale_made, 1)
            pe.wait_ge(xw_copied, NCH)
            nc.tensor.matmul(n_ps[0:D, 0:D], w_t[0:D, :], diag_s[0:D, :], start=True, stop=True)\
                .then_inc(set_pe, 1)
            pass1(1, False, True)
            with pe.Fori(2, NCH) as ic:
                pass1(ic, False)

            def pass2(ic, deferred):
                g = NCH + ic - 1
                for q in range(NP):
                    if deferred == 2 and q in BLOCKS:
                        product_block(ic - 2, BLOCKS[q])
                    if q == 0:
                        m_acc_free(NCH + ic)
                        if deferred == 0:
                            pe.wait_ge(s_mid_made, NCH - 1)
                    if deferred == 0 and q == NP - KT // 2:
                        pe.wait_ge(s_mid_made, NCH)
                    product(ic, q, q, s_mid, 1)
                    if deferred == 0 and q == 0:
                        counts(NCH - 1, NQ - 1, False)
                    if q == P2_GATES:
                        gates(g, 1 if deferred else 0,
                              [(h_made, g), (sup_made, ic - 1) if deferred == 2 else
                               (s_mid_made, NCH - 1 + deferred)])
                    if q == P2_NODE:
                        node(g, 1 if deferred else 0)
                    if deferred:
                        if q == P2_X1T:
                            x1_turn(ic - 1)
                        if q == P2_SUP:
                            support(ic - 1)

            pass2(0, 0)
            pass2(1, 1)
            pe.wait_ge(codes_made, 2 * NCH * NQ)
            with pe.Fori(2, NCH) as ic:
                pass2(ic, 2)

            product_block(NCH - 2, 0)
            gates(2 * NCH - 1, 1, [(h_made, 2 * NCH - 1), (sup_made, NCH - 1)])
            for b in range(1, NCH - 2):
                product_block(NCH - 2, b)
            node(2 * NCH - 1, 1)
            product_block(NCH - 2, NCH - 2)
            x1_turn(NCH - 1)
            product_block(NCH - 2, NCH - 1)
            support(NCH - 1)

            def turn(b):
                pe.wait_ge(acc_added, (NCH - 1) * NCH + b + 1 + ACC_READY)
                if b >= 4:
                    pe.wait_ge(y_made, b - 3)
                for k in range(KT):
                    last = nc.tensor.matmul(turn_ps[b % 4][:, k * D:(k + 1) * D],
                                            out_acc[:, b * CW + k * P:b * CW + (k + 1) * P],
                                            unscale[:, :], start=True, stop=True)
                last.then_inc(turned, 1)

            for b in range(NCH):
                product_block(NCH - 1, b, at_end=True)
                if b > 0:
                    turn(b - 1)
            turn(NCH - 1)

        @block.scalar
        def _(act):
            act.dma_start(w12[D:P, :], w2).then_inc(consts_loaded, 16)
            for half in range(2):
                act.dma_start(w_t[half * D:(half + 1) * D, :], weight_t).then_inc(consts_loaded, 16)
            act.wait_ge(set_pool, SET_POOL)
            for i, (wih, whh, bi, bh) in enumerate(((wih1_t, whh1_t, bih1, bhh1),
                                                    (wih2_t, whh2_t, bih2, bhh2))):
                act.dma_start(w_rz[i][0:D, :], wih[:, 0:P]).then_inc(consts_loaded, 16)
                act.dma_start(w_rz[i][D:P, :], whh[:, 0:P]).then_inc(consts_loaded, 16)
                act.dma_start(w_n[i][0:D, D:P], wih[:, P:3 * D]).then_inc(consts_loaded, 16)
                act.dma_start(w_n[i][D:P, 0:D], whh[:, P:3 * D]).then_inc(consts_loaded, 16)
                act.dma_start(b_i[:, i:i + 1], bi[0:P, :]).then_inc(consts_loaded, 16)
                act.dma_start(b_h[:, i:i + 1], bh[0:P, :]).then_inc(consts_loaded, 16)
                act.dma_start(b_n[0:D, i:i + 1], bh[P:3 * D, :]).then_inc(consts_loaded, 16)
                act.dma_start(b_n[D:P, i:i + 1], bi[P:3 * D, :]).then_inc(consts_loaded, 16)
            act.dma_start(bias_b[:, :, :], bias).then_inc(consts_loaded, 16)

            def code(ic, qd):
                act.wait_ge(cnt_done, ic * NQ + qd + 1)
                for w in (1, 0):
                    at = (NQ - 1 - qd) * QW + w * PW
                    nc.scalar.activation(codes[:, bass.ds(ic * (NT * CW) + at, PW)], cnt[w][:, :],
                                         ACT.Relu, bias=code_bias[:, :]).then_inc(codes_made, 1)

            def high(g, first):
                act.wait_ge(pair_used, (g + 1) * NP)
                if not first:
                    act.wait_ge(m_ready, g)
                nc.scalar.activation(m_high, m_acc[D:P, :], ACT.Copy).then_inc(high_copied, 1)

            def sigmoids(g, layer, first):
                act.wait_ge(gates_done, g + 1)
                if not first:
                    act.wait_ge(d_made, 3 * g)
                nc.scalar.activation(rz[:, :], rz_ps[:, :], ACT.Sigmoid,
                                     bias=b_rz[:, layer:layer + 1]).then_inc(rz_made, 1)

            def tanh(g, layer):
                act.wait_ge(t_made, 2 * (g + 1))
                nc.scalar.activation(n_g, t_n, ACT.Tanh,
                                     bias=b_n[D:P, layer:layer + 1]).then_inc(n_made, 1)

            def relu(g, first, stored=None, store_to=None):
                act.wait_ge(d_made, 3 * (g + 1))
                if not first:
                    act.wait_ge(node_done, g)
                if stored is not None:
                    act.wait_ge(h_stored, stored)
                nc.scalar.activation(h_c[D:P, :], t_n, ACT.Relu).then_inc(h_made, 1)
                if store_to is not None:
                    act.wait_ge(h_made, g + 1)
                    act.dma_start(store_to, h_c[D:P, :]).then_inc(h_stored, 16)

            def square(c, first):
                act.wait_ge(node_done, NCH + c + 1)
                if not first:
                    act.wait_ge(sums_of_sq, c)
                nc.scalar.activation(sq[:, :, :], nodes(node_ps), ACT.Square).then_inc(sq_made, 1)

            def x1_turned(c):
                act.wait_ge(x1t_done, c + 1)
                nc.scalar.activation(x1_t, node_ps[0:D, :], ACT.Copy).then_inc(x1t_copied, 1)

            def split_high(c, first):
                act.wait_ge(sup_done, c + 1)
                if not first:
                    act.wait_ge(block_done, c * NCH)
                nc.scalar.activation(sup[:, :, 0, :], nodes(node_ps), ACT.Copy)\
                    .then_inc(sup_high, 1)

            def expand(c, b, early=False):
                if not early:
                    act.wait_ge(block_done, c * NCH + b - 1)
                nc.scalar.activation(wexp[:, b % 2, :].bitcast(U16),
                                     codes[:, bass.ds(c * (KT * CW) + b * NT * CW, KT * CW)],
                                     ACT.Copy, scale=float(P)).then_inc(wexp_made[0], 1)

            def expand_last(b):
                c = NCH - 1
                if b == 0:
                    act.wait_ge(pair_used, 2 * NCH * NP)
                at = c * KT * CW + b * NT * CW
                nc.scalar.activation(last_w[:, b, :].bitcast(U16), codes[:, at:at + KT * CW],
                                     ACT.Copy, scale=float(P)).then_inc(last_w_made[0], 1)

            def pass1(ic, first, second=False):
                for qd in range(NQ):
                    if not first and qd == 0:
                        high(ic - 1, second)
                        code(ic - 1, NQ - 2)
                    elif not first and qd == 1:
                        code(ic - 1, NQ - 1)
                    elif qd > 1:
                        code(ic, qd - 2)
                    if not first:
                        if qd == P1_SIG:
                            sigmoids(ic - 1, 0, second)
                        if qd == P1_TANH:
                            tanh(ic - 1, 0)
                        if qd == P1_RELU:
                            relu(ic - 1, second, None if second else 16 * (ic - 1),
                                 h_dram[:, bass.ts(ic - 1, CW)])

            pass1(0, True)
            act.wait_ge(set_dve, 4)
            pass1(1, False, True)
            with act.Fori(2, NCH) as ic:
                pass1(ic, False)

            def pass2(ic, deferred):
                g = NCH + ic - 1
                layer = 1 if deferred else 0
                for q in range(NP):
                    if q == 0:
                        high(g, False)
                        if deferred == 0:
                            code(NCH - 1, NQ - 2)
                            code(NCH - 1, NQ - 1)
                    if q == P2_SIG:
                        sigmoids(g, layer, False)
                    if q == P2_TANH:
                        tanh(g, layer)
                    if q == P2_RELU:
                        if deferred == 0:
                            relu(g, False, 16 * (NCH - 1), h_dram[:, bass.ts(NCH - 1, CW)])
                        else:
                            relu(g, False, 16 * NCH if deferred == 1 else None)
                    if deferred:
                        if q == P2_SQUARE:
                            square(ic - 1, deferred == 1)
                        if q == P2_X1T:
                            x1_turned(ic - 1)
                        if q == P2_SPLIT:
                            split_high(ic - 1, deferred == 1)
                    if deferred == 2 and q in BLOCKS and BLOCKS[q] % 2 and BLOCKS[q] < NCH - 1:
                        expand(ic - 2, BLOCKS[q] + 1)
                if deferred:
                    expand(ic - 1, 0, deferred == 1)

            pass2(0, 0)
            pass2(1, 1)
            with act.Fori(2, NCH) as ic:
                pass2(ic, 2)
            g = 2 * NCH - 1
            high(g, False)
            expand(NCH - 2, 2)
            sigmoids(g, 1, False)
            expand(NCH - 2, 4)
            tanh(g, 1)
            expand(NCH - 2, 6)
            relu(g, False)
            square(NCH - 1, False)
            expand_last(0)
            x1_turned(NCH - 1)
            split_high(NCH - 1, False)
            for b in range(2, NCH, 2):
                expand_last(b)

            def square_last(b):
                act.wait_ge(y_made, b + 1)
                if b >= 2:
                    act.wait_ge(sums_of_sq, NCH + b - 1)
                nc.scalar.activation(ysq[:, b % 2], y[:, b % 4], ACT.Square).then_inc(sq_made, 1)

            for b in range(NCH):
                square_last(b)

        @block.gpsimd
        def _(pool):
            for i in range(2):
                nc.gpsimd.memset(w_n[i][:, :], 0.0).then_inc(set_pool, 1)
            nc.gpsimd.memset(ident[:, :], 0.0).then_inc(set_pool, 1)
            nc.gpsimd.memset(tri[:, :], -1.0).then_inc(set_pool, 1)
            nc.gpsimd.memset(neg_ones[:, :], -1.0).then_inc(set_pool, 1)
            nc.gpsimd.memset(code_bias[:, :], float(NEIGH - BIG)).then_inc(set_pool, 1)
            nc.gpsimd.memset(mhalf[:, :], -0.5).then_inc(set_pool, 1)
            nc.gpsimd.memset(centre[:, :], -1.0 / D).then_inc(set_pool, 1)
            pool.wait_ge(set_pool, 8)
            nc.gpsimd.affine_select(out=ident[:, :], in_=ident[:, :], compare_op=ALU.not_equal,
                                    fill=1.0, base=0, pattern=[[-1, P]],
                                    channel_multiplier=1).then_inc(set_pool, 1)
            nc.gpsimd.affine_select(out=tri[:, :], in_=tri[:, :], compare_op=ALU.is_gt, fill=0.0,
                                    base=0, pattern=[[-1, P]], channel_multiplier=1)\
                .then_inc(set_pool, 1)
            pool.wait_ge(set_pool, 10)
            nc.gpsimd.affine_select(out=tri[:, :], in_=tri[:, :], compare_op=ALU.not_equal,
                                    fill=float(BIG), base=0, pattern=[[-1, P]],
                                    channel_multiplier=1).then_inc(set_pool, 1)
            nc.gpsimd.memset(stat[:, :, :], 0.0).then_inc(set_pool, 1)
            pool.wait_ge(cnt_done, NCH * NQ)
            pool.wait_ge(rsum_made, NCH * RSUMS)
            nc.gpsimd.memset(out_acc, 0.0).then_inc(acc_added, ACC_READY)

            def to_rstd(c, r):
                pool.wait_ge(var_made, c + 1)
                nc.gpsimd.tensor_tensor(rstd[:, r, :], var[:, r, :], mhalf[:, :], ALU.pow)\
                    .then_inc(rstd_made, 1)

            def add_bias(c):
                pool.wait_ge(x1_made, c + 1)
                nc.gpsimd.tensor_tensor(xb[:, :, :], x1[:, :, :], bias_b[:, :, :], ALU.add)\
                    .then_inc(xb_made, 1)

            to_rstd(0, 0)
            add_bias(0)
            with pool.Fori(1, NCH) as c:
                to_rstd(c, 0)
                pool.wait_ge(x1b_made, c)
                add_bias(c)
            for b in range(NCH):
                to_rstd(NCH + b, b % 4)

        @block.vector
        def _(dve):
            def xw_copy(u):
                c = NCH - 1 - u
                dve.wait_ge(xw_done, u + 1)
                nc.vector.tensor_copy(s_in[:, c * KT * D:(c + 1) * KT * D],
                                      (rz_ps, n_ps)[u % 2][:, 0:KT * D]).then_inc(xw_copied, 1)

            def constants():
                dve.wait_ge(consts_loaded, 16 * 20)
                nc.vector.tensor_reduce(w_max[:, 0:1], w_t[:, :], AX_X, ALU.max,
                                        apply_absolute_value=True).then_inc(set_dve, 1)
                dve.wait_ge(set_dve, 1)
                nc.vector.tensor_scalar(w_max[:, 1:2], w_max[:, 0:1], 2.0 ** -100, None, ALU.max)\
                    .then_inc(set_dve, 1)
                dve.wait_ge(set_dve, 2)
                nc.vector.tensor_scalar(w_max[:, 2:3].bitcast(I32), w_max[:, 1:2].bitcast(I32),
                                        0x7F800000, None, ALU.bitwise_and).then_inc(set_dve, 1)
                nc.vector.tensor_tensor(b_rz[:, :], b_i[:, :], b_h[:, :], ALU.add)\
                    .then_inc(set_dve, 1)
                dve.wait_ge(set_dve, 3)
                nc.vector.tensor_scalar(w_max[:, 3:4].bitcast(I32), w_max[:, 2:3].bitcast(I32),
                                        -1.0, 254.0 * EXP_ONE, ALU.mult, ALU.add)\
                    .then_inc(set_dve, 1)
                dve.wait_ge(set_pool, SET_POOL)
                for rows in (slice(0, D), slice(D, P)):
                    nc.vector.tensor_copy(ident2[rows, :], ident[rows, rows]).then_inc(set_dve, 1)
                dve.wait_ge(set_dve, 7)
                nc.vector.tensor_tensor(centre[:, :], centre[:, :], ident2[:, :], ALU.add)\
                    .then_inc(set_dve, 1)
                nc.vector.tensor_scalar(diag_s[:, :], ident2[:, :], w_max[:, 3:4], 2.0 ** 8,
                                        ALU.mult, ALU.mult).then_inc(scale_made, 1)
                dve.wait_ge(set_dve, 8)
                nc.vector.tensor_scalar(unscale[:, :], centre[:, :], w_max[:, 2:3],
                                        2.0 ** (CODE_SHIFT - 8), ALU.mult, ALU.mult)\
                    .then_inc(set_dve, 1)

            def mask(ic, q, early):
                dve.wait_ge(adj_in[q % SLOTS], 16 * (ic * (NP // SLOTS) + q // SLOTS + 1))
                if not early and q % 2 == 0:
                    dve.wait_ge(cnt_done, ic * NQ + q // 2 - 1)
                at = (q // 2 % 2) * QW + (1 - q % 2) * PW
                nc.vector.tensor_scalar(masks[:, at:at + PW], stream[:, q % SLOTS, :],
                                        0.0, None, ALU.not_equal).then_inc(mask_made, 1)

            def running_sums(ic, qd):
                r, b = qd % 2, (qd - 1) % 2
                m = [masks[:, r * QW + u * CW:r * QW + (u + 1) * CW] for u in range(4)]
                s = [rsums[:, r * QW + u * CW:r * QW + (u + 1) * CW] for u in range(4)]
                m_before, s_before = masks[:, b * QW:b * QW + CW], rsums[:, b * QW:b * QW + CW]
                n = ic * RSUMS + (4 * qd - 2 if qd else 0)
                if qd == 0:
                    steps = [(s[1], m[3], m[2]), (s[0], s[1], m[1])]
                else:
                    steps = [(s[3], s_before, m_before), (s[2], s[3], m[3]), (s[1], s[2], m[2]),
                             (s[0], s[1], m[1])]
                for k, (to, a, c) in enumerate(steps):
                    if qd or k:
                        dve.wait_ge(rsum_made, n + k)
                    if k == (1 if qd else 0):
                        dve.wait_ge(mask_made, ic * NP + 2 * qd + 2)
                    nc.vector.tensor_tensor(to, a, c, ALU.add).then_inc(rsum_made, 1)

            def low(g, first):
                dve.wait_ge(pair_used, (g + 1) * NP)
                if not first:
                    dve.wait_ge(gates_done, g)
                nc.vector.tensor_copy(mx[0:D, :], m_acc[0:D, :]).then_inc(low_copied, 1)

            def add_halves(g):
                dve.wait_ge(low_copied, g + 1)
                dve.wait_ge(high_copied, g + 1)
                nc.vector.tensor_tensor(mx[0:D, :], mx[0:D, :], m_high, ALU.add)\
                    .then_inc(m_ready, 1)

            def n_input(g, layer, first):
                dve.wait_ge(rz_made, g + 1)
                if not first:
                    dve.wait_ge(h_made, g)
                nc.vector.scalar_tensor_tensor(t_n, n_ps[0:D, :], b_n[0:D, layer:layer + 1],
                                               rz[0:D, :], ALU.add, ALU.mult).then_inc(t_made, 1)
                dve.wait_ge(t_made, 2 * g + 1)
                nc.vector.tensor_tensor(t_n, t_n, n_ps[D:P, :], ALU.add).then_inc(t_made, 1)

            def new_h(g):
                dve.wait_ge(n_made, g + 1)
                nc.vector.tensor_tensor(t_n, mx[D:P, :], n_g, ALU.subtract).then_inc(d_made, 1)
                dve.wait_ge(d_made, 3 * g + 1)
                nc.vector.tensor_tensor(t_n, t_n, rz[D:P, :], ALU.mult).then_inc(d_made, 1)
                dve.wait_ge(d_made, 3 * g + 2)
                nc.vector.tensor_tensor(t_n, t_n, n_g, ALU.add).then_inc(d_made, 1)

            def to_s_mid(c):
                dve.wait_ge(node_done, c + 1)
                nc.vector.tensor_copy(s_mid[:, bass.ts(c, KT * D)], node_ps[:, 0:KT * D])\
                    .then_inc(s_mid_made, 1)

            def pass1(ic, first, second=False):
                for qd in range(NQ):
                    for q in (2 * qd, 2 * qd + 1):
                        mask(ic, q, first and qd < 2)
                        if not first and q == 0:
                            add_halves(ic - 1)
                    if qd == NQ - 1:
                        low(ic, first)
                    if first and qd < NQ - 1:
                        xw_copy(qd + 1)
                    running_sums(ic, qd)
                    if first and qd == 5:
                        constants()
                    if not first:
                        if qd == P1_T:
                            n_input(ic - 1, 0, second)
                        if qd == P1_H:
                            new_h(ic - 1)
                        if qd == P1_OUT:
                            to_s_mid(ic - 1)

            xw_copy(0)
            pass1(0, True)
            dve.wait_ge(set_pe, 1)
            nc.vector.tensor_copy(w_s[:, :], n_ps[0:D, 0:D]).then_inc(w_s_made, 1)
            pass1(1, False, True)
            with dve.Fori(2, NCH) as ic:
                pass1(ic, False)

            def variance(n, r, src):
                dve.wait_ge(sq_made, n + 1)
                nc.vector.tensor_reduce(stat[:, r, :], src, AX_X, ALU.add).then_inc(sums_of_sq, 1)
                dve.wait_ge(sums_of_sq, n + 1)
                nc.vector.tensor_scalar(var[:, r, :], stat[:, r, :], 1.0 / D, EPS,
                                        ALU.mult, ALU.add).then_inc(var_made, 1)

            def norm(c, first):
                variance(c, 0, sq[:, :, :])
                dve.wait_ge(rstd_made, c + 1)
                if not first:
                    dve.wait_ge(xb_made, c)
                    dve.wait_ge(x1t_done, c)
                nc.vector.tensor_tensor(x1[:, :, :], nodes(node_ps),
                                        rstd[:, 0, :].unsqueeze(2).to_broadcast([P, KT, D]),
                                        ALU.mult).then_inc(x1_made, 1)

            def centre_x1b(c):
                dve.wait_ge(xb_made, c + 1)
                nc.vector.tensor_reduce(stat[:, 1, :], xb[:, :, :], AX_X, ALU.add)\
                    .then_inc(centred, 1)
                dve.wait_ge(centred, 2 * c + 1)
                nc.vector.tensor_scalar(stat[:, 2, :], stat[:, 1, :], -1.0 / D, None, ALU.mult)\
                    .then_inc(centred, 1)
                dve.wait_ge(centred, 2 * c + 2)
                nc.vector.tensor_tensor(
                    x1b[:, bass.ts(c, KT * D)].rearrange("p (k d) -> p k d", d=D), xb[:, :, :],
                    stat[:, 2, :].unsqueeze(2).to_broadcast([P, KT, D]), ALU.add)\
                    .then_inc(x1b_made, 1)

            def split_low(c):
                dve.wait_ge(sup_high, c + 1)
                nc.vector.tensor_tensor(sup[:, :, 1, :], nodes(node_ps), sup[:, :, 0, :],
                                        ALU.subtract).then_inc(sup_made, 1)

            def expand(c, b):
                nc.vector.tensor_scalar(wexp[:, b % 2, :].bitcast(U16),
                                        codes[:, bass.ds(c * (KT * CW) + b * NT * CW, KT * CW)],
                                        float(P), None, ALU.mult).then_inc(wexp_made[1], 1)

            def expand_last(b):
                if b == 1:
                    dve.wait_ge(pair_used, 2 * NCH * NP)
                at = (NCH - 1) * KT * CW + b * NT * CW
                nc.vector.tensor_scalar(last_w[:, b, :].bitcast(U16), codes[:, at:at + KT * CW],
                                        float(P), None, ALU.mult).then_inc(last_w_made[1], 1)

            def accumulate(c, b):
                dve.wait_ge(block_done, c * NCH + b + 1)
                at = out_acc[:, b * CW:(b + 1) * CW]
                nc.vector.tensor_tensor(at, out_ps[b % 4], at, ALU.add).then_inc(acc_added, 1)

            def pass2(ic, deferred):
                g = NCH + ic - 1
                layer = 1 if deferred else 0
                for q in range(NP):
                    if q == 0:
                        if deferred:
                            low(g, False)
                        add_halves(g)
                    if q == P2_T:
                        n_input(g, layer, False)
                    if q == P2_H:
                        new_h(g)
                    if deferred == 0 and q == P2_NODE:
                        to_s_mid(NCH - 1)
                    if deferred and q == P2_NORM:
                        norm(ic - 1, deferred == 1)
                    if deferred and q == P2_SPLIT:
                        split_low(ic - 1)
                    if deferred and q == P2_CENTER:
                        centre_x1b(ic - 1)
                    if deferred == 2 and q in BLOCKS:
                        if BLOCKS[q] % 2 == 0:
                            expand(ic - 2, BLOCKS[q] + 1)
                        accumulate(ic - 2, BLOCKS[q])
                if deferred == 1:
                    dve.wait_ge(acc_added, ACC_READY)

            pass2(0, 0)
            pass2(1, 1)
            with dve.Fori(2, NCH) as ic:
                pass2(ic, 2)
            g = 2 * NCH - 1
            low(g, False)
            add_halves(g)
            dve.wait_ge(block_done, (NCH - 2) * NCH)
            expand(NCH - 2, 1)
            expand_last(1)
            n_input(g, 1, False)
            accumulate(NCH - 2, 0)
            new_h(g)
            accumulate(NCH - 2, 1)
            expand(NCH - 2, 3)
            accumulate(NCH - 2, 2)
            accumulate(NCH - 2, 3)
            expand(NCH - 2, 5)
            variance(NCH - 1, 0, sq[:, :, :])
            dve.wait_ge(rstd_made, NCH)
            dve.wait_ge(xb_made, NCH - 1)
            dve.wait_ge(x1t_done, NCH - 1)
            nc.vector.tensor_tensor(x1[:, :, :], nodes(node_ps),
                                    rstd[:, 0, :].unsqueeze(2).to_broadcast([P, KT, D]),
                                    ALU.mult).then_inc(x1_made, 1)
            accumulate(NCH - 2, 4)
            accumulate(NCH - 2, 5)
            expand(NCH - 2, 7)
            accumulate(NCH - 2, 6)
            split_low(NCH - 1)
            accumulate(NCH - 2, NCH - 1)
            for b in range(3, NCH, 2):
                expand_last(b)
            centre_x1b(NCH - 1)

            def add_x1(b):
                dve.wait_ge(turned, b + 1)
                if b == 0:
                    dve.wait_ge(x1b_made, NCH)
                if b >= 4:
                    dve.wait_ge(o_made, b - 3)
                nc.vector.tensor_tensor(
                    y[:, b % 4], nodes(turn_ps[b % 4]),
                    x1b[:, b * KT * D:(b + 1) * KT * D].rearrange("p (k d) -> p k d", d=D),
                    ALU.add).then_inc(y_made, 1)

            def scale_out(b):
                dve.wait_ge(rstd_made, NCH + b + 1)
                if b >= 2:
                    dve.wait_ge(out_stored[b % 2], 16 * (b // 2))
                nc.vector.tensor_tensor(o_n[:, b % 2], y[:, b % 4],
                                        rstd[:, b % 4, :].unsqueeze(2).to_broadcast([P, KT, D]),
                                        ALU.mult).then_inc(o_made, 1)

            for i in range(NCH + 3):
                if i < NCH:
                    accumulate(NCH - 1, i)
                if 1 <= i <= NCH:
                    add_x1(i - 1)
                if 2 <= i <= NCH + 1:
                    variance(NCH + i - 2, (i - 2) % 4, ysq[:, i % 2])
                if i >= 3:
                    scale_out(i - 3)


def kernel(x, adj, L0_gnn_W1, L0_gnn_wih1, L0_gnn_whh1, L0_gnn_bih1, L0_gnn_bhh1, L0_gnn_W2,
           L0_gnn_wih2, L0_gnn_whh2, L0_gnn_bih2, L0_gnn_bhh2, L1_gnn_weight, L1_gnn_bias):
    import numpy as np
    import concourse.bacc as bacc
    from concourse.bass_utils import run_bass_kernel_spmd

    adj_t = np.ascontiguousarray(
        np.asarray(adj).reshape(NCH, CW, NP, 2, P).transpose(0, 2, 4, 3, 1)).reshape(NCH, NP, P, PW)
    arrays = {
        "adj_t": adj_t,
        "x_t": np.ascontiguousarray(np.asarray(x).T),
        "w1": np.ascontiguousarray(L0_gnn_W1),
        "w2": np.ascontiguousarray(L0_gnn_W2),
        "wih1_t": np.ascontiguousarray(np.asarray(L0_gnn_wih1).T),
        "whh1_t": np.ascontiguousarray(np.asarray(L0_gnn_whh1).T),
        "wih2_t": np.ascontiguousarray(np.asarray(L0_gnn_wih2).T),
        "whh2_t": np.ascontiguousarray(np.asarray(L0_gnn_whh2).T),
        "bih1": np.ascontiguousarray(L0_gnn_bih1).reshape(3 * D, 1),
        "bhh1": np.ascontiguousarray(L0_gnn_bhh1).reshape(3 * D, 1),
        "bih2": np.ascontiguousarray(L0_gnn_bih2).reshape(3 * D, 1),
        "bhh2": np.ascontiguousarray(L0_gnn_bhh2).reshape(3 * D, 1),
        "weight_t": np.ascontiguousarray(np.asarray(L1_gnn_weight).T),
        "bias": np.ascontiguousarray(L1_gnn_bias).reshape(1, D),
    }
    nc = bacc.Bacc("TRN2", target_bir_lowering=False, num_devices=1, dynamic_dma_scratch_size=1024)
    aps = {name: nc.dram_tensor(f"in_{name}", a.shape, mybir.dt.from_np(a.dtype),
                                kind="ExternalInput").ap() for name, a in arrays.items()}
    out = nc.dram_tensor("out_nodes", (N, D), F32, kind="ExternalOutput").ap()
    h_dram = nc.dram_tensor("h_dram", (D, N), F32, kind="Internal").ap()
    aps["bias"] = aps["bias"].unsqueeze(1).to_broadcast([P, KT, D])
    build(nc, out=out.rearrange("(c k p) d -> c p k d", k=KT, p=P), h_dram=h_dram, **aps)
    r = run_bass_kernel_spmd(nc, [{f"in_{name}": a for name, a in arrays.items()}], core_ids=[0])
    return r.results[0]["out_nodes"]
```

```python
from contextlib import ExitStack

import concourse.bass as bass
from concourse import mybir

F32 = mybir.dt.float32
BF16 = mybir.dt.bfloat16
F16 = mybir.dt.float16
U8 = mybir.dt.uint8
U16 = mybir.dt.uint16
I32 = mybir.dt.int32
ALU = mybir.AluOpType
ACT = mybir.ActivationFunctionType
AX_X = mybir.AxisListType.X

P = 128
N = 4096
D = 64
CW = 512
NCH = N // CW
KT = CW // P
NT = N // P
NP = NT // 2
NQ = NT // 4
PW = 2 * CW
QW = 4 * CW
SLOTS = 8
NEIGH = 100
BIG = 128
CODE_SHIFT = 27
EXP_ONE = 1 << 23
EPS = 1e-5
RSUMS = NT - 2
LATE_CHUNKS = 2
LATE = 4
LATE_RSUMS = 4 * LATE - 1
SET_POOL = 12
ACC_READY = 4

P1_GATES, P1_SIG, P1_T, P1_TANH, P1_H, P1_RELU, P1_NODE, P1_OUT = 0, 1, 2, 3, 4, 5, 5, 6
P2_GATES, P2_SIG, P2_T, P2_TANH, P2_H, P2_RELU, P2_NODE = 1, 2, 3, 4, 5, 6, 7
P2_SQUARE, P2_NORM, P2_SPLIT, P2_CENTER = 8, 9, 14, 15
BLOCKS = {0: 0, 2: 1, 4: 2, 6: 3, 8: 4, 10: 5, 12: 6, 13: 7}

LAST_ACT = [(6, 0), (6, 2), (6, 4), (6, 6), (7, 0), (7, 2), (7, 1), (7, 3), (7, 4), (7, 6)]
LAST_DVE = [(6, 7), (6, 1), (6, 3), (6, 5), (7, 5), (7, 7)]
LAST_ACT_STEPS, LAST_DVE_STEPS = [1, 3, 5, 7, 9, 12], [1, 6, 10, 12]

AT_RZ, AT_N, AT_W2, AT_WT = 0, 2 * P, 4 * P, 4 * P + D
AT_BI, AT_BH, AT_BN = AT_WT + D, AT_WT + D + 2, AT_WT + D + 4
CONSTS = AT_BN + 2

BY_ACT = 4

LATE_MASKS, LATE_SUMS = {0: 4, 1: 5, 6: 6, 9: 7}, {0: 4, 5: 5, 7: 6, 10: 7}
LATE_COUNTS, LATE_CODES = {3: 4, 8: 5, 10: 6, 12: 7}, {4: 4, 9: 5, 11: 6, 13: 7}


def halved(ic):
    return isinstance(ic, int) and ic < LATE_CHUNKS


def quads_before(ic, qd, late=False):
    if late:
        return NCH * NQ - (LATE_CHUNKS - ic) * LATE + qd - (NQ - LATE)
    if halved(ic):
        return ic * (NQ - LATE) + qd
    return ic * NQ - LATE_CHUNKS * LATE + qd


def masks_before(ic, qd, late=False):
    passed_over = 2 * LATE * (ic if halved(ic) and not late else LATE_CHUNKS)
    return 2 * quads_before(ic, qd, late) + passed_over


def sums_before(ic, qd, late=False):
    within = 4 * qd - 2 if qd else 0
    if late:
        return (NCH * RSUMS - (LATE_CHUNKS - ic) * LATE_RSUMS
                + (4 * (qd - NQ + LATE) - 1 if qd > NQ - LATE else 0))
    if halved(ic):
        return ic * (RSUMS - LATE_RSUMS) + within
    return ic * RSUMS - LATE_CHUNKS * LATE_RSUMS + within


def late_start(qd, late):
    return late and qd == NQ - LATE


def late_pair(q):
    return NP // 2 - 1 - q if q < NP // 2 else q


def build(nc, adj_t, x_t, x_pairs, w1, consts, bias, out, h_dram):
    with ExitStack() as ctx:
        def sb(name, shape, dt):
            return ctx.enter_context(nc.sbuf_tensor(name, shape, dt))

        def sem(name):
            return ctx.enter_context(nc.semaphore(name))

        codes = sb("codes", [P, NCH * NT * CW], U8)
        x_sb = codes[:, (NCH - 1) * NT * CW:(NCH - 1) * NT * CW + N * 2].bitcast(F32)
        stream = sb("stream", [P, SLOTS, PW], F32)
        y, ysq, o_n = [stream[:, 2 * i:2 * i + 2, :].rearrange("p s (b k d) -> p (s b) k d",
                                                               k=KT, d=D) for i in range(3)]
        s_in = sb("s_in", [P, NT * D], F32)
        x1b = s_in
        s_mid = sb("s_mid", [P, NT * D], F32)
        shared = sb("shared", [P, NCH * CW], F32)
        out_acc = shared[:, :]
        masks = shared[:, 0:QW].bitcast(BF16)
        rsums = shared[:, QW:2 * QW].bitcast(BF16)
        wexp = sb("wexp", [P, 2, KT * CW], BF16)
        carry = [sb("carry", [P, CW], BF16)[:, :], wexp[:, 1, 0:CW]]
        mx = sb("mx", [P, CW], F32)
        m_high_t = sb("m_high_t", [P, CW], F32)
        m_high = m_high_t[0:D, :]
        t_n = m_high_t[D:P, :]
        rz = sb("rz", [P, CW], F32)
        n_g = sb("n_t", [P, CW], F32)[D:P, :]
        h_c = sb("h_c", [P, CW], F32)
        sq = sb("sq", [P, KT, D], F32)
        x1s = sb("x1s", [P, KT, 2, D], F32)
        x1, sup_f = x1s[:, :, 0, :], x1s[:, :, 1, :]
        xb = sb("xb", [P, KT, D], F32)
        stat = sb("stat", [P, NCH, KT], F32)
        var = sb("var", [P, NCH, KT], F32)
        rstd = sb("rstd", [P, NCH, KT], F32)
        mhalf = sb("mhalf", [P, KT], F32)
        sup = sb("sup", [P, KT, 2, D], F16)
        const = sb("const", [P, CONSTS], F32)
        w_rz = [const[:, AT_RZ + i * P:AT_RZ + (i + 1) * P] for i in range(2)]
        w_n = [const[:, AT_N + i * P:AT_N + (i + 1) * P] for i in range(2)]
        w_2 = const[:, AT_W2:AT_W2 + D]
        w_t = const[:, AT_WT:AT_WT + D]
        b_i, b_h, b_n = [const[:, at:at + 2] for at in (AT_BI, AT_BH, AT_BN)]
        w_1 = sb("w_1", [P, P], F32)
        b_rz = sb("b_rz", [P, 2], F32)
        ones_f = sb("ones_f", [D, P], F32)
        w_max = sb("w_max", [P, 4], F32)
        unscale = sb("unscale", [P, 1], F32)
        centre_s = sb("centre_s", [P, D], F32)
        w_s = sb("w_s", [D, D], F32)
        bias_b = sb("bias_b", [P, KT, D], F32)
        ident2 = sb("ident2", [P, D], F32)
        to_x1s = sb("to_x1s", [P, 2 * D], F32)
        centre, to_sup = to_x1s[:, 0:D], to_x1s[:, D:2 * D]
        tri = sb("tri", [P, P], BF16)
        neg_ones = sb("neg_ones", [P, P], BF16)
        no_mask = sb("no_mask", [P, 1], F32)
        code_bias = sb("code_bias", [P, 1], F32)

        m_acc, rz_ps, n_ps, spare_ps = [
            ctx.enter_context(nc.psum_tensor(f"bank{i}", [P, CW], F32)) for i in range(4)]
        node_ps = rz_ps
        cnt = [ctx.enter_context(nc.psum_tensor(f"wide{i}", [P, PW], F32)) for i in range(2)]
        out_ps = [cnt[0][:, 0:CW], cnt[1][:, 0:CW], cnt[0][:, CW:PW], cnt[1][:, CW:PW]]
        end_ps = out_ps + [spare_ps, m_acc, n_ps, rz_ps]

        def acc_part(b, part):
            return out_acc[:, b * CW:(b + 1) * CW].rearrange("p (t h d) -> p t h d", h=2, d=D)[
                :, :, part, :]

        def last_w(c, b):
            at = b * NT * CW + (c - (NCH - 2)) * 2 * KT * CW
            return codes[:, at:at + 2 * KT * CW].bitcast(BF16)

        def halves(ps):
            return ps[:, :].rearrange("p (k h d) -> p k h d", h=2, d=D)

        x_in = [sem(f"x_in{i}") for i in range(NCH)]
        w1_in, consts_loaded = sem("w1_in"), sem("consts_loaded")
        adj_in = [sem(f"adj_in{i}") for i in range(SLOTS)]
        pair_used, mask_made, rsum_made = sem("pair_used"), sem("mask_made"), sem("rsum_made")
        cnt_done, codes_made = sem("cnt_done"), sem("codes_made")
        xw_done, xw_copied = sem("xw_done"), sem("xw_copied")
        high_copied, low_copied, m_ready = sem("high_copied"), sem("low_copied"), sem("m_ready")
        state_in, rz_done, gates_done = sem("state_in"), sem("rz_done"), sem("gates_done")
        rz_made = sem("rz_made")
        t_made, n_made, d_made, h_made = sem("t_made"), sem("n_made"), sem("d_made"), sem("h_made")
        h_stored, node_done, s_mid_made = sem("h_stored"), sem("node_done"), sem("s_mid_made")
        x_c_in, sq_made, sums_of_sq = sem("x_c_in"), sem("sq_made"), sem("sums_of_sq")
        var_made, rstd_made, x1_made = sem("var_made"), sem("rstd_made"), sem("x1_made")
        xb_made, centred, x1b_made = sem("xb_made"), sem("centred"), sem("x1b_made")
        sup_high, sup_made, held_done = sem("sup_high"), sem("sup_made"), sem("held_done")
        wexp_made = [sem(f"wexp_made{i}") for i in range(2)]
        last_by_act, last_by_dve = sem("last_by_act"), sem("last_by_dve")
        block_done, acc_zeroed, acc_added = sem("block_done"), sem("acc_zeroed"), sem("acc_added")
        parts_summed, base_made = sem("parts_summed"), sem("base_made")
        half_made, y_made = sem("half_made"), sem("y_made")
        o_by_act, o_by_dve = sem("o_by_act"), sem("o_by_dve")
        out_stored = sem("out_stored")
        set_pool, set_dve, scale_made = sem("set_pool"), sem("set_dve"), sem("scale_made")
        w_max_made, bound_done = sem("w_max_made"), sem("bound_done")
        w_s_done, w_s_made, to_sup_done = sem("w_s_done"), sem("w_s_made"), sem("to_sup_done")
        to_sup_made = sem("to_sup_made")

        block = ctx.enter_context(nc.Block())

        @block.sync
        def _(sp):
            def slot_free(freed, masked):
                sp.wait_ge(pair_used, freed)
                if masked is not None:
                    sp.wait_ge(mask_made, masked)

            def load(q, src):
                sp.dma_start(stream[:, q % SLOTS, :], src).then_inc(adj_in[q % SLOTS], 16)

            def load_x(u):
                at = slice((NCH - 1 - u) * 2 * P, (NCH - u) * 2 * P)
                sp.dma_start(x_sb[:, at], x_pairs[:, at]).then_inc(x_in[u], 16)

            def state(g, src):
                if g is not None:
                    sp.wait_ge(d_made, g)
                sp.dma_start(mx[D:P, :], src).then_inc(state_in, 16)

            def pass1(ic, first):
                for q in range(NP):
                    if not first or q >= SLOTS:
                        freed = ic * NP + q - SLOTS + 1
                        slot_free(freed, freed)
                    if q == NP - 1:
                        state(None if first else 3 * ic - 2, x_t[:, bass.ts(ic, CW)])
                    load(q, adj_t[ic, NP - 1 - q])
                    if first and q % 2 == 0 and q < NP - 2:
                        load_x(q // 2 + 1)
                    if first and q == 4:
                        sp.dma_start(const[:, :], consts).then_inc(consts_loaded, 16)
                        sp.dma_start(bias_b[:, :, :], bias).then_inc(consts_loaded, 16)

            def pass2(ic, first):
                for q in range(NP):
                    freed = (NCH + ic) * NP + q - SLOTS + 1
                    masked = halved(ic) and (ic == 0 or q >= SLOTS)
                    slot_free(freed, freed - 2 * LATE * ic if masked else None)
                    if q == NP - 1:
                        sp.wait_ge(h_stored, 16 * (ic + 1))
                        state(3 * (NCH + ic) - 2, h_dram[:, bass.ts(ic, CW)])
                        if not first:
                            sp.wait_ge(node_done, NCH + ic)
                        sp.dma_start(h_c[0:D, :], x_t[:, bass.ts(ic, CW)]).then_inc(x_c_in, 16)
                    load(q, adj_t[ic, late_pair(q) if halved(ic) else q])

            sp.dma_start(w_1[:, :], w1).then_inc(w1_in, 16)
            load_x(0)
            pass1(0, True)
            with sp.Fori(1, NCH) as ic:
                pass1(ic, False)
            pass2(0, True)
            pass2(1, False)
            with sp.Fori(2, NCH) as ic:
                pass2(ic, False)
            for b in range(NCH):
                if b < BY_ACT:
                    sp.wait_ge(o_by_act, b + 1)
                else:
                    sp.wait_ge(o_by_dve, b + 1 - BY_ACT)
                sp.dma_start(out[b], o_n[:, b]).then_inc(out_stored, 16)
            sp.wait_ge(out_stored, 16 * NCH)
            sp.wait_ge(h_stored, 16 * NCH)

        @block.tensor
        def _(pe):
            def x_w1(u):
                pe.wait_ge(x_in[u], 16)
                if u == 0:
                    pe.wait_ge(w1_in, 16)
                if u >= 2:
                    pe.wait_ge(xw_copied, u - 1)
                c = NCH - 1 - u
                for k in range(2):
                    last = nc.tensor.matmul((rz_ps, n_ps)[u % 2][:, k * P:(k + 1) * P],
                                            x_sb[:, (c * 2 + k) * P:(c * 2 + k + 1) * P],
                                            w_1[:, :], start=True, stop=True)
                last.then_inc(xw_done, 1)

            def product(ic, q, pair, s, npass):
                pe.wait_ge(adj_in[q % SLOTS],
                           16 * ((ic + npass * NCH) * (NP // SLOTS) + q // SLOTS + 1))
                for u in range(2):
                    t = 2 * pair + u
                    last = nc.tensor.matmul(m_acc[D * u:D * (u + 1), :], s[:, t * D:(t + 1) * D],
                                            stream[:, q % SLOTS, u * CW:(u + 1) * CW],
                                            start=(q == 0), stop=(q == NP - 1))
                last.then_inc(pair_used, 1)

            def counts(ic, qd, early, late=False):
                r, before = qd % 2, quads_before(ic, qd, late)
                pe.wait_ge(mask_made, masks_before(ic, qd, late) + 2)
                m = [masks[:, r * QW + u * CW:r * QW + (u + 1) * CW] for u in range(4)]
                s = [rsums[:, r * QW + u * CW:r * QW + (u + 1) * CW] for u in range(4)]
                if qd == 0:
                    s[3], s[2] = None, m[3]
                elif late_start(qd, late):
                    s[3] = carry[ic]
                pe.wait_ge(rsum_made, sums_before(ic, qd, late)
                           + (2 if qd == 0 else 3 if late_start(qd, late) else 4))
                for u in (3, 2, 1, 0):
                    if not early and u % 2:
                        pe.wait_ge(codes_made, 2 * before - (1 if u == 3 else 0))
                    to = cnt[u // 2][:, (u % 2) * CW:(u % 2 + 1) * CW]
                    last = nc.tensor.matmul(to, tri[:, :], m[u], start=True, stop=s[u] is None)
                    if s[u] is not None:
                        last = nc.tensor.matmul(to, neg_ones[:, :], s[u], start=False, stop=True)
                last.then_inc(cnt_done, 1)

            def gates(g, layer, free):
                pe.wait_ge(m_ready, g + 1)
                pe.wait_ge(state_in, 16 * (g + 1))
                for f in free:
                    pe.wait_ge(*f)
                nc.tensor.matmul(rz_ps[:, :], w_rz[layer], mx[:, :], start=True, stop=True)\
                    .then_inc(rz_done, 1)
                nc.tensor.matmul(n_ps[:, :], w_n[layer], mx[:, :], start=True, stop=True)\
                    .then_inc(gates_done, 1)

            def node(g, layer):
                pe.wait_ge(h_made, g + 1)
                if layer:
                    pe.wait_ge(x_c_in, 16 * (g - NCH + 1))
                lo, rhs = (0, to_x1s) if layer else (D, w_2)
                n = 2 * D if layer else D
                for k in range(KT):
                    last = nc.tensor.matmul(node_ps[:, k * n:(k + 1) * n],
                                            h_c[lo:P, k * P:(k + 1) * P], rhs[lo:P, :],
                                            start=True, stop=True)
                last.then_inc(node_done, 1)

            def share(to, w, start, stop):
                for t in range(KT):
                    for k in range(KT):
                        last = nc.tensor.matmul(to[:, t * P:(t + 1) * P],
                                                w[:, k * CW + t * P:k * CW + (t + 1) * P],
                                                sup[:, k, :, :], start=start and t + k == 0,
                                                stop=stop and t + k == 2 * KT - 2)
                return last

            def product_block(c, b):
                if b == 0:
                    pe.wait_ge(sup_made, c + 1)
                pe.wait_ge(wexp_made[b % 2], c * (NCH // 2) + b // 2 + 1)
                pe.wait_ge(acc_added, c * NCH + b - 3 + ACC_READY)
                share(out_ps[b % 4], wexp[:, b % 2, :], True, True).then_inc(block_done, 1)

            def last_block(c, b, to, start, stop):
                if (c, b) in LAST_ACT:
                    pe.wait_ge(last_by_act, LAST_ACT.index((c, b)) + 1)
                else:
                    pe.wait_ge(last_by_dve, LAST_DVE.index((c, b)) + 1)
                return share(to, last_w(c, b), start, stop)

            def m_acc_free(g):
                pe.wait_ge(high_copied, g)
                pe.wait_ge(low_copied, g)

            def pass1(ic, first, second=False):
                for qd in range(NQ):
                    if qd == 0 and not first:
                        m_acc_free(ic)
                    if first and qd < NQ - 1 and qd > 0:
                        x_w1(qd + 1)
                    if first:
                        pe.wait_ge(xw_copied, qd + 1)
                    for q in (2 * qd, 2 * qd + 1):
                        product(ic, q, NP - 1 - q, s_in, 0)
                    if first and qd == 0:
                        x_w1(1)
                    if first and qd == 5:
                        pe.wait_ge(w_max_made, 1)
                        nc.tensor.matmul(spare_ps[:, 0:1], ones_f[:, :], w_max[0:D, 0:1],
                                         start=True, stop=True).then_inc(bound_done, 1)
                    if 0 < qd <= (NQ - LATE if halved(ic) else NQ):
                        counts(ic, qd - 1, first and qd == 1)
                    elif qd == 0 and not first and not halved(ic - 1):
                        counts(ic - 1, NQ - 1, False)
                    if not first:
                        if qd == P1_GATES:
                            gates(ic - 1, 0, [] if second else
                                  [(h_made, ic - 1), (s_mid_made, ic - 1)])
                        if qd == P1_NODE + second:
                            node(ic - 1, 0)
                    if second and qd == 1:
                        pe.wait_ge(scale_made, 1)
                        nc.tensor.matmul(spare_ps[0:D, 0:D], w_t[0:D, :], centre_s[0:D, :],
                                         start=True, stop=True).then_inc(w_s_done, 1)
                    if second and qd == 5:
                        pe.wait_ge(w_s_made, 1)
                        for rows in (slice(0, D), slice(D, P)):
                            last = nc.tensor.matmul(spare_ps[rows, D:2 * D], centre[0:D, :],
                                                    w_s[:, :], start=True, stop=True)
                        last.then_inc(to_sup_done, 1)

            x_w1(0)
            pe.wait_ge(set_pool, SET_POOL)
            pass1(0, True)
            pass1(1, False, True)
            pass1(2, False)
            with pe.Fori(3, NCH) as ic:
                pass1(ic, False)

            def pass2(ic, deferred):
                g = NCH + ic - 1
                for q in range(NP):
                    if deferred >= 2 and q in BLOCKS:
                        product_block(ic - 2, BLOCKS[q])
                    if q == 0:
                        m_acc_free(NCH + ic)
                        if deferred == 0:
                            pe.wait_ge(s_mid_made, NCH - 1)
                    if deferred == 0 and q == NP - KT // 2:
                        pe.wait_ge(s_mid_made, NCH)
                    product(ic, q, late_pair(q) if halved(ic) else q, s_mid, 1)
                    if deferred == 0 and q == 1:
                        counts(NCH - 1, NQ - 1, False)
                    if halved(ic) and q in LATE_COUNTS:
                        counts(ic, LATE_COUNTS[q], False, True)
                    if q == P2_GATES:
                        gates(g, 1 if deferred else 0,
                              [(h_made, g), (x1_made, ic - 1) if deferred >= 2 else
                               (s_mid_made, NCH - 1 + deferred)])
                    if q == P2_NODE:
                        node(g, 1 if deferred else 0)

            pass2(0, 0)
            pass2(1, 1)
            pe.wait_ge(codes_made, 2 * NCH * NQ)
            with pe.Fori(2, NCH - 1) as ic:
                pass2(ic, 2)
            pass2(NCH - 1, 3)

            c, g = NCH - 2, 2 * NCH - 1
            pe.wait_ge(sup_made, c + 1)
            last_block(c, 7, spare_ps, True, True).then_inc(block_done, 1)
            gates(g, 1, [(h_made, g), (x1_made, c + 1)])
            for b in range(4):
                pe.wait_ge(acc_added, c * NCH + b - 3 + ACC_READY)
                last_block(c, b, end_ps[b], True, False)
            m_acc_free(g + 1)
            last_block(c, 5, end_ps[5], True, False)
            pe.wait_ge(acc_added, c * NCH + 1 + ACC_READY)
            last_block(c, 4, end_ps[4], True, False)
            node(g, 1)
            pe.wait_ge(t_made, 2 * (g + 1))
            pe.wait_ge(sums_of_sq, NCH)
            last_block(c, 6, end_ps[6], True, False).then_inc(held_done, 1)
            pe.wait_ge(sup_made, NCH)
            for b in range(NCH):
                last_block(NCH - 1, b, end_ps[b], b == NCH - 1, True).then_inc(block_done, 1)

        @block.scalar
        def _(act):
            def code(ic, qd, late=False):
                act.wait_ge(cnt_done, quads_before(ic, qd, late) + 1)
                for w in (1, 0):
                    at = (NQ - 1 - qd) * QW + w * PW
                    nc.scalar.activation(codes[:, bass.ds(ic * (NT * CW) + at, PW)], cnt[w][:, :],
                                         ACT.Relu, bias=code_bias[:, :]).then_inc(codes_made, 1)

            def high(g, first):
                act.wait_ge(pair_used, (g + 1) * NP)
                if not first:
                    act.wait_ge(m_ready, g)
                nc.scalar.activation(m_high, m_acc[D:P, :], ACT.Copy).then_inc(high_copied, 1)

            def sigmoids(g, layer, first):
                act.wait_ge(rz_done, g + 1)
                if not first:
                    act.wait_ge(d_made, 3 * g)
                nc.scalar.activation(rz[:, :], rz_ps[:, :], ACT.Sigmoid,
                                     bias=b_rz[:, layer:layer + 1]).then_inc(rz_made, 1)

            def tanh(g, layer):
                act.wait_ge(t_made, 2 * (g + 1))
                nc.scalar.activation(n_g, t_n, ACT.Tanh,
                                     bias=b_n[D:P, layer:layer + 1]).then_inc(n_made, 1)

            def relu(g, first, stored=None, store_to=None):
                act.wait_ge(d_made, 3 * (g + 1))
                if not first:
                    act.wait_ge(node_done, g)
                if stored is not None:
                    act.wait_ge(h_stored, stored)
                nc.scalar.activation(h_c[D:P, :], t_n, ACT.Relu).then_inc(h_made, 1)
                if store_to is not None:
                    act.wait_ge(h_made, g + 1)
                    act.dma_start(store_to, h_c[D:P, :]).then_inc(h_stored, 16)

            def square(c, first):
                act.wait_ge(node_done, NCH + c + 1)
                if not first:
                    act.wait_ge(sums_of_sq, c)
                nc.scalar.activation(sq[:, :, :], halves(node_ps)[:, :, 0, :], ACT.Square)\
                    .then_inc(sq_made, 1)

            def split_high(c, first):
                act.wait_ge(x1_made, c + 1)
                if not first:
                    if c < NCH - 1:
                        act.wait_ge(block_done, c * NCH)
                    else:
                        act.wait_ge(held_done, 1)
                nc.scalar.activation(sup[:, :, 0, :], sup_f, ACT.Copy).then_inc(sup_high, 1)

            def expand(c, b, early=False):
                if not early:
                    act.wait_ge(block_done, c * NCH + b - 1)
                nc.scalar.activation(wexp[:, b % 2, :].bitcast(U16),
                                     codes[:, bass.ds(c * (KT * CW) + b * NT * CW, KT * CW)],
                                     ACT.Copy, scale=float(P)).then_inc(wexp_made[0], 1)

            def expand_last(n):
                c, b = LAST_ACT[n]
                at = c * KT * CW + b * NT * CW
                nc.scalar.activation(last_w(c, b).bitcast(U16), codes[:, at:at + KT * CW],
                                     ACT.Copy, scale=float(P)).then_inc(last_by_act, 1)

            def pass1(ic, first, second=False):
                for qd in range(NQ):
                    if not first and qd == 0:
                        high(ic - 1, second)
                    if not first and not halved(ic - 1) and qd < 2:
                        code(ic - 1, NQ - 2 + qd)
                    if 1 < qd < (NQ - LATE + 2 if halved(ic) else NQ):
                        code(ic, qd - 2)
                    if not first:
                        if qd == P1_SIG:
                            sigmoids(ic - 1, 0, second)
                        if qd == P1_TANH:
                            tanh(ic - 1, 0)
                        if qd == P1_RELU:
                            relu(ic - 1, second, None if second else 16 * (ic - 1),
                                 h_dram[:, bass.ts(ic - 1, CW)])

            pass1(0, True)
            act.wait_ge(set_dve, 3)
            pass1(1, False, True)
            pass1(2, False)
            with act.Fori(3, NCH) as ic:
                pass1(ic, False)

            def pass2(ic, deferred):
                g = NCH + ic - 1
                layer = 1 if deferred else 0
                for q in range(NP):
                    if q == 0:
                        high(g, False)
                        if deferred == 0:
                            code(NCH - 1, NQ - 2)
                            code(NCH - 1, NQ - 1)
                    if q == P2_SIG:
                        sigmoids(g, layer, False)
                    if q == P2_TANH:
                        tanh(g, layer)
                    if halved(ic) and q in LATE_CODES:
                        code(ic, LATE_CODES[q], True)
                    if q == P2_RELU:
                        if deferred == 0:
                            relu(g, False, 16 * (NCH - 1), h_dram[:, bass.ts(NCH - 1, CW)])
                        else:
                            relu(g, False, 16 * NCH if deferred == 1 else None)
                    if deferred:
                        if q == P2_SQUARE:
                            square(ic - 1, deferred == 1)
                        if q == P2_SPLIT:
                            split_high(ic - 1, deferred == 1)
                    b = BLOCKS.get(q + 1, 0)
                    if deferred >= 2 and b % 2 and b < NCH - 1:
                        expand(ic - 2, b + 1)
                    if deferred == 3 and q in LAST_ACT_STEPS:
                        expand_last(LAST_ACT_STEPS.index(q))
                    if deferred == 1 and q == P2_NODE:
                        expand(0, 0, True)
                if deferred == 2:
                    expand(ic - 1, 0)

            pass2(0, 0)
            pass2(1, 1)
            with act.Fori(2, NCH - 1) as ic:
                pass2(ic, 2)
            pass2(NCH - 1, 3)
            g = 2 * NCH - 1
            high(g, False)
            sigmoids(g, 1, False)
            expand_last(6)
            tanh(g, 1)
            expand_last(7)
            relu(g, False)
            square(NCH - 1, False)
            expand_last(8)
            split_high(NCH - 1, False)
            expand_last(9)

            for i in range(NCH):
                act.wait_ge(y_made, i + 1)
                nc.scalar.activation(ysq[:, i], y[:, i], ACT.Square).then_inc(sq_made, 1)
                b = i - 3
                if 0 <= b < BY_ACT:
                    act.wait_ge(rstd_made, NCH + b + 1)
                    for k in range(KT):
                        last = nc.scalar.activation(o_n[:, b, k, :], y[:, b, k, :],
                                                    ACT.Copy, scale=rstd[:, b, k:k + 1])
                    last.then_inc(o_by_act, 1)

        @block.gpsimd
        def _(pool):
            nc.gpsimd.memset(ident2[:, :], 0.0).then_inc(set_pool, 1)
            nc.gpsimd.memset(tri[:, :], -1.0).then_inc(set_pool, 1)
            nc.gpsimd.memset(neg_ones[:, :], -1.0).then_inc(set_pool, 1)
            nc.gpsimd.memset(code_bias[:, :], float(NEIGH - BIG)).then_inc(set_pool, 1)
            nc.gpsimd.memset(mhalf[:, :], -0.5).then_inc(set_pool, 1)
            nc.gpsimd.memset(centre, -1.0 / D).then_inc(set_pool, 1)
            pool.wait_ge(set_pool, 6)
            nc.gpsimd.affine_select(out=ident2[:, :], in_=ident2[:, :], compare_op=ALU.not_equal,
                                    fill=1.0, base=0, pattern=[[-1, D]],
                                    channel_multiplier=1).then_inc(set_pool, 1)
            nc.gpsimd.affine_select(out=tri[:, :], in_=tri[:, :], compare_op=ALU.is_gt, fill=0.0,
                                    base=0, pattern=[[-1, P]], channel_multiplier=1)\
                .then_inc(set_pool, 1)
            pool.wait_ge(set_pool, 8)
            nc.gpsimd.affine_select(out=ident2[:, :], in_=ident2[:, :], compare_op=ALU.not_equal,
                                    fill=1.0, base=-D, pattern=[[-1, D]],
                                    channel_multiplier=1).then_inc(set_pool, 1)
            nc.gpsimd.affine_select(out=tri[:, :], in_=tri[:, :], compare_op=ALU.not_equal,
                                    fill=float(BIG), base=0, pattern=[[-1, P]],
                                    channel_multiplier=1).then_inc(set_pool, 1)
            nc.gpsimd.memset(stat[:, :, :], 0.0).then_inc(set_pool, 1)
            nc.gpsimd.memset(ones_f[:, :], 1.0).then_inc(set_pool, 1)

            def to_rstd(c, r):
                pool.wait_ge(var_made, c + 1)
                nc.gpsimd.tensor_tensor(rstd[:, r, :], var[:, r, :], mhalf[:, :], ALU.pow)\
                    .then_inc(rstd_made, 1)

            def add_bias(c):
                pool.wait_ge(x1_made, c + 1)
                nc.gpsimd.tensor_tensor(xb[:, :, :], x1, bias_b[:, :, :], ALU.add)\
                    .then_inc(xb_made, 1)

            to_rstd(0, 0)
            add_bias(0)
            pool.wait_ge(cnt_done, NCH * NQ)
            pool.wait_ge(rsum_made, NCH * RSUMS)
            nc.gpsimd.memset(out_acc, 0.0).then_inc(acc_zeroed, 1)
            with pool.Fori(1, NCH - 1) as c:
                to_rstd(c, 0)
                pool.wait_ge(x1b_made, c)
                add_bias(c)
            for b in range(NCH):
                pool.wait_ge(acc_added, (NCH - 2) * NCH + (b == NCH - 1) + ACC_READY)
                nc.gpsimd.tensor_tensor(acc_part(b, 0), acc_part(b, 0), acc_part(b, 1), ALU.add)\
                    .then_inc(parts_summed, 1)
            to_rstd(NCH - 1, 0)
            pool.wait_ge(x1b_made, NCH - 1)
            add_bias(NCH - 1)
            for b in range(NCH):
                to_rstd(NCH + b, b)

        @block.vector
        def _(dve):
            def xw_copy(u):
                c = NCH - 1 - u
                dve.wait_ge(xw_done, u + 1)
                at = s_in[:, c * KT * D:(c + 1) * KT * D]
                nc.vector.tensor_copy(
                    at.rearrange("p (h k d) -> p k h d", h=2, k=2),
                    (rz_ps, n_ps)[u % 2][:, 0:KT * D].rearrange("p (k h d) -> p k h d", h=2, k=2))\
                    .then_inc(xw_copied, 1)

            def weight_max():
                dve.wait_ge(consts_loaded, 16 * 2)
                nc.vector.tensor_reduce(w_max[0:D, 0:1], w_t[0:D, :], AX_X, ALU.max,
                                        apply_absolute_value=True).then_inc(w_max_made, 1)

            def constants():
                dve.wait_ge(bound_done, 1)
                nc.vector.tensor_scalar(w_max[:, 1:2], spare_ps[:, 0:1], 2.0 ** -100, None,
                                        ALU.max).then_inc(set_dve, 1)
                dve.wait_ge(set_dve, 1)
                nc.vector.tensor_scalar(w_max[:, 2:3].bitcast(I32), w_max[:, 1:2].bitcast(I32),
                                        0x7F800000, None, ALU.bitwise_and).then_inc(set_dve, 1)
                nc.vector.tensor_tensor(b_rz[:, :], b_i, b_h, ALU.add)\
                    .then_inc(set_dve, 1)
                dve.wait_ge(set_dve, 2)
                nc.vector.tensor_scalar(w_max[:, 3:4].bitcast(I32), w_max[:, 2:3].bitcast(I32),
                                        -1.0, 254.0 * EXP_ONE, ALU.mult, ALU.add)\
                    .then_inc(set_dve, 1)
                dve.wait_ge(set_pool, SET_POOL)
                nc.vector.tensor_tensor(centre, centre, ident2[:, :], ALU.add)\
                    .then_inc(set_dve, 1)
                dve.wait_ge(set_dve, 5)
                nc.vector.tensor_scalar(centre_s[:, :], centre, w_max[:, 3:4], 2.0 ** 7,
                                        ALU.mult, ALU.mult).then_inc(scale_made, 1)
                nc.vector.tensor_scalar(unscale[:, :], w_max[:, 2:3], 2.0 ** (CODE_SHIFT - 7),
                                        None, ALU.mult).then_inc(set_dve, 1)

            def mask(ic, q, early, late=False):
                dve.wait_ge(adj_in[q % SLOTS], 16 * ((NCH + ic) * (NP // SLOTS) + 1) if late else
                            16 * (ic * (NP // SLOTS) + q // SLOTS + 1))
                if not early and q % 2 == 0:
                    dve.wait_ge(cnt_done, quads_before(ic, q // 2, late) - 1)
                at = (q // 2 % 2) * QW + (1 - q % 2) * PW
                nc.vector.tensor_scalar(masks[:, at:at + PW], stream[:, q % SLOTS, :],
                                        0.0, None, ALU.not_equal).then_inc(mask_made, 1)

            def running_sums(ic, qd, late=False):
                r, b = qd % 2, (qd - 1) % 2
                m = [masks[:, r * QW + u * CW:r * QW + (u + 1) * CW] for u in range(4)]
                s = [rsums[:, r * QW + u * CW:r * QW + (u + 1) * CW] for u in range(4)]
                m_before, s_before = masks[:, b * QW:b * QW + CW], rsums[:, b * QW:b * QW + CW]
                n = sums_before(ic, qd, late)
                if qd == 0:
                    steps = [(s[1], m[3], m[2]), (s[0], s[1], m[1])]
                elif late_start(qd, late):
                    steps = [(s[2], carry[ic], m[3]), (s[1], s[2], m[2]), (s[0], s[1], m[1])]
                else:
                    steps = [(s[3], s_before, m_before), (s[2], s[3], m[3]), (s[1], s[2], m[2]),
                             (s[0], s[1], m[1])]
                for k, (to, a, c) in enumerate(steps):
                    if qd or k:
                        dve.wait_ge(rsum_made, n + k)
                    if k == (0 if qd == 0 or late_start(qd, late) else 1):
                        dve.wait_ge(mask_made, masks_before(ic, qd, late) + 2)
                    nc.vector.tensor_tensor(to, a, c, ALU.add).then_inc(rsum_made, 1)

            def pass_over():
                nc.vector.memset(no_mask[:, :], 0.0).then_inc(mask_made, 2 * LATE)

            def to_carry(ic):
                dve.wait_ge(rsum_made, sums_before(ic, NQ - LATE))
                at = (NQ - LATE - 1) % 2 * QW
                nc.vector.tensor_tensor(carry[ic], rsums[:, at:at + CW], masks[:, at:at + CW],
                                        ALU.add).then_inc(rsum_made, 1)

            def low(g, first):
                dve.wait_ge(pair_used, (g + 1) * NP)
                if not first:
                    dve.wait_ge(gates_done, g)
                nc.vector.tensor_copy(mx[0:D, :], m_acc[0:D, :]).then_inc(low_copied, 1)

            def add_halves(g):
                dve.wait_ge(low_copied, g + 1)
                dve.wait_ge(high_copied, g + 1)
                nc.vector.tensor_tensor(mx[0:D, :], mx[0:D, :], m_high, ALU.add)\
                    .then_inc(m_ready, 1)

            def n_input(g, layer, first):
                dve.wait_ge(rz_made, g + 1)
                dve.wait_ge(gates_done, g + 1)
                if not first:
                    dve.wait_ge(h_made, g)
                nc.vector.scalar_tensor_tensor(t_n, n_ps[0:D, :], b_n[0:D, layer:layer + 1],
                                               rz[0:D, :], ALU.add, ALU.mult).then_inc(t_made, 1)
                dve.wait_ge(t_made, 2 * g + 1)
                nc.vector.tensor_tensor(t_n, t_n, n_ps[D:P, :], ALU.add).then_inc(t_made, 1)

            def new_h(g):
                dve.wait_ge(n_made, g + 1)
                nc.vector.tensor_tensor(t_n, mx[D:P, :], n_g, ALU.subtract).then_inc(d_made, 1)
                dve.wait_ge(d_made, 3 * g + 1)
                nc.vector.tensor_tensor(t_n, t_n, rz[D:P, :], ALU.mult).then_inc(d_made, 1)
                dve.wait_ge(d_made, 3 * g + 2)
                nc.vector.tensor_tensor(t_n, t_n, n_g, ALU.add).then_inc(d_made, 1)

            def to_s_mid(c):
                dve.wait_ge(node_done, c + 1)
                nc.vector.tensor_copy(s_mid[:, bass.ts(c, KT * D)], node_ps[:, 0:KT * D])\
                    .then_inc(s_mid_made, 1)

            def pass1(ic, first, second=False):
                for qd in range(NQ):
                    for q in (2 * qd, 2 * qd + 1):
                        if not halved(ic) or qd < NQ - LATE:
                            mask(ic, q, first and qd < 2)
                        if not first and q == 0:
                            add_halves(ic - 1)
                    if qd == NQ - 1:
                        low(ic, first)
                    if first and qd < NQ - 1:
                        xw_copy(qd + 1)
                    if not halved(ic) or qd < NQ - LATE:
                        running_sums(ic, qd)
                    if halved(ic) and qd == NQ - LATE:
                        to_carry(ic)
                        pass_over()
                    if first and qd == 4:
                        weight_max()
                    if first and qd == 6:
                        constants()
                    if not first:
                        if qd == P1_T:
                            n_input(ic - 1, 0, second)
                        if qd == P1_H:
                            new_h(ic - 1)
                        if qd == P1_OUT + second:
                            to_s_mid(ic - 1)
                    if second and qd == 3:
                        dve.wait_ge(w_s_done, 1)
                        nc.vector.tensor_copy(w_s[:, :], spare_ps[0:D, 0:D]).then_inc(w_s_made, 1)
                    if second and qd == 6:
                        dve.wait_ge(to_sup_done, 1)
                        nc.vector.tensor_copy(to_sup, spare_ps[:, D:2 * D])\
                            .then_inc(to_sup_made, 1)

            nc.vector.memset(no_mask[:, :], 0.0).then_inc(acc_added, ACC_READY)
            xw_copy(0)
            pass1(0, True)
            pass1(1, False, True)
            pass1(2, False)
            with dve.Fori(3, NCH) as ic:
                pass1(ic, False)

            def sum_squares(n, r, src):
                dve.wait_ge(sq_made, n + 1)
                nc.vector.tensor_reduce(stat[:, r, :], src, AX_X, ALU.add).then_inc(sums_of_sq, 1)

            def add_eps(n, r):
                dve.wait_ge(sums_of_sq, n + 1)
                nc.vector.tensor_scalar(var[:, r, :], stat[:, r, :], 1.0 / D, EPS,
                                        ALU.mult, ALU.add).then_inc(var_made, 1)

            def variance(n, r, src):
                sum_squares(n, r, src)
                add_eps(n, r)

            def make_x1s():
                nc.vector.tensor_tensor(x1s[:, :, :, :].rearrange("p k h d -> p k (h d)"),
                                        node_ps[:, :].rearrange("p (k n) -> p k n", k=KT),
                                        rstd[:, 0, :].unsqueeze(2).to_broadcast([P, KT, 2 * D]),
                                        ALU.mult).then_inc(x1_made, 1)

            def norm(c, first):
                variance(c, 0, sq[:, :, :])
                dve.wait_ge(rstd_made, c + 1)
                if not first:
                    dve.wait_ge(xb_made, c)
                    dve.wait_ge(sup_made, c)
                make_x1s()

            def centre_x1b(c):
                dve.wait_ge(xb_made, c + 1)
                nc.vector.tensor_reduce(stat[:, 1, :], xb[:, :, :], AX_X, ALU.add)\
                    .then_inc(centred, 1)
                dve.wait_ge(centred, 2 * c + 1)
                nc.vector.tensor_scalar(stat[:, 2, :], stat[:, 1, :], -1.0 / D, None, ALU.mult)\
                    .then_inc(centred, 1)
                dve.wait_ge(centred, 2 * c + 2)
                nc.vector.tensor_tensor(
                    x1b[:, bass.ts(c, KT * D)].rearrange("p (k d) -> p k d", d=D), xb[:, :, :],
                    stat[:, 2, :].unsqueeze(2).to_broadcast([P, KT, D]), ALU.add)\
                    .then_inc(x1b_made, 1)

            def split_low(c):
                dve.wait_ge(sup_high, c + 1)
                nc.vector.tensor_tensor(sup[:, :, 1, :], sup_f, sup[:, :, 0, :],
                                        ALU.subtract).then_inc(sup_made, 1)

            def expand(c, b):
                nc.vector.tensor_scalar(wexp[:, b % 2, :].bitcast(U16),
                                        codes[:, bass.ds(c * (KT * CW) + b * NT * CW, KT * CW)],
                                        float(P), None, ALU.mult).then_inc(wexp_made[1], 1)

            def expand_last(n):
                c, b = LAST_DVE[n]
                at = c * KT * CW + b * NT * CW
                nc.vector.tensor_scalar(last_w(c, b).bitcast(U16), codes[:, at:at + KT * CW],
                                        float(P), None, ALU.mult).then_inc(last_by_dve, 1)

            def accumulate(c, b):
                dve.wait_ge(block_done, c * NCH + b + 1)
                at = out_acc[:, b * CW:(b + 1) * CW]
                nc.vector.tensor_tensor(at, out_ps[b % 4], at, ALU.add).then_inc(acc_added, 1)

            def pass2(ic, deferred):
                g = NCH + ic - 1
                layer = 1 if deferred else 0
                for q in range(NP):
                    if q == 0:
                        if deferred:
                            low(g, False)
                        add_halves(g)
                    if q == P2_T:
                        n_input(g, layer, False)
                    if q == P2_H:
                        new_h(g)
                    if deferred == 0 and q == P2_NODE:
                        to_s_mid(NCH - 1)
                    if halved(ic) and q in LATE_SUMS and q > 0:
                        running_sums(ic, LATE_SUMS[q], True)
                    if halved(ic) and q in LATE_MASKS:
                        for pair in (2 * LATE_MASKS[q], 2 * LATE_MASKS[q] + 1):
                            mask(ic, pair, False, True)
                    if halved(ic) and q == 0:
                        running_sums(ic, LATE_SUMS[q], True)
                    if deferred and q == P2_NORM:
                        norm(ic - 1, deferred == 1)
                    if deferred and q == P2_SPLIT:
                        split_low(ic - 1)
                    if deferred and q == P2_CENTER:
                        centre_x1b(ic - 1)
                    if deferred >= 2 and q in BLOCKS:
                        if BLOCKS[q] % 2 == 0:
                            expand(ic - 2, BLOCKS[q] + 1)
                        accumulate(ic - 2, BLOCKS[q])
                    if deferred == 3 and q in LAST_DVE_STEPS:
                        expand_last(LAST_DVE_STEPS.index(q))
                if deferred == 1:
                    dve.wait_ge(acc_zeroed, 1)

            pass2(0, 0)
            pass2(1, 1)
            with dve.Fori(2, NCH - 1) as ic:
                pass2(ic, 2)
            pass2(NCH - 1, 3)

            def x1b_nodes(b):
                return x1b[:, b * KT * D:(b + 1) * KT * D].rearrange("p (k d) -> p k d", d=D)

            def base(b):
                dve.wait_ge(parts_summed, b + 1)
                dve.wait_ge(x1b_made, b + 1)
                nc.vector.scalar_tensor_tensor(x1b_nodes(b), acc_part(b, 0), unscale[:, 0:1],
                                               x1b_nodes(b), ALU.mult, ALU.add)\
                    .then_inc(base_made, 1)

            g = 2 * NCH - 1
            low(g, False)
            add_halves(g)
            dve.wait_ge(block_done, (NCH - 2) * NCH + 1)
            at = out_acc[:, (NCH - 1) * CW:NCH * CW]
            nc.vector.tensor_tensor(at, spare_ps[:, :], at, ALU.add).then_inc(acc_added, 1)
            base(0)
            n_input(g, 1, False)
            expand_last(4)
            new_h(g)
            expand_last(5)
            base(1)
            base(2)
            base(3)
            variance(NCH - 1, 0, sq[:, :, :])
            base(4)
            base(5)
            dve.wait_ge(rstd_made, NCH)
            dve.wait_ge(xb_made, NCH - 1)
            make_x1s()
            base(6)
            split_low(NCH - 1)
            centre_x1b(NCH - 1)

            def end_part(b, part):
                return halves(end_ps[b])[:, :, part, :]

            def scale_out(b):
                dve.wait_ge(rstd_made, NCH + b + 1)
                nc.vector.tensor_tensor(o_n[:, b], y[:, b],
                                        rstd[:, b, :].unsqueeze(2).to_broadcast([P, KT, D]),
                                        ALU.mult).then_inc(o_by_dve, 1)

            for i in range(NCH + 1):
                if i == 1:
                    base(7)
                if i < NCH:
                    dve.wait_ge(block_done, (NCH - 2) * NCH + i + 2)
                    dve.wait_ge(base_made, i + 1)
                    nc.vector.scalar_tensor_tensor(x1b_nodes(i), end_part(i, 0), unscale[:, 0:1],
                                                   x1b_nodes(i), ALU.mult, ALU.add)\
                        .then_inc(half_made, 1)
                if i >= 1:
                    sum_squares(NCH + i - 1, i - 1, ysq[:, i - 1])
                if i < NCH:
                    dve.wait_ge(half_made, i + 1)
                    nc.vector.scalar_tensor_tensor(y[:, i], end_part(i, 1), unscale[:, 0:1],
                                                   x1b_nodes(i), ALU.mult, ALU.add)\
                        .then_inc(y_made, 1)
                if i >= 1:
                    add_eps(NCH + i - 1, i - 1)
                if i - 3 >= BY_ACT:
                    scale_out(i - 3)
            for b in range(NCH - 2, NCH):
                scale_out(b)


def kernel(x, adj, L0_gnn_W1, L0_gnn_wih1, L0_gnn_whh1, L0_gnn_bih1, L0_gnn_bhh1, L0_gnn_W2,
           L0_gnn_wih2, L0_gnn_whh2, L0_gnn_bih2, L0_gnn_bhh2, L1_gnn_weight, L1_gnn_bias):
    import numpy as np
    import concourse.bacc as bacc
    from concourse.bass_utils import run_bass_kernel_spmd

    adj_t = np.ascontiguousarray(
        np.asarray(adj).reshape(NCH, CW, NP, 2, P).transpose(0, 2, 4, 3, 1)).reshape(NCH, NP, P, PW)
    consts = np.zeros((P, CONSTS), np.float32)
    for i, (wih, whh, bi, bh) in enumerate((
            (L0_gnn_wih1, L0_gnn_whh1, L0_gnn_bih1, L0_gnn_bhh1),
            (L0_gnn_wih2, L0_gnn_whh2, L0_gnn_bih2, L0_gnn_bhh2))):
        wih_t, whh_t = np.asarray(wih).T, np.asarray(whh).T
        consts[0:D, AT_RZ + i * P:AT_RZ + (i + 1) * P] = wih_t[:, 0:P]
        consts[D:P, AT_RZ + i * P:AT_RZ + (i + 1) * P] = whh_t[:, 0:P]
        consts[0:D, AT_N + i * P + D:AT_N + (i + 1) * P] = wih_t[:, P:3 * D]
        consts[D:P, AT_N + i * P:AT_N + i * P + D] = whh_t[:, P:3 * D]
        consts[:, AT_BI + i], consts[:, AT_BH + i] = bi[0:P], bh[0:P]
        consts[0:D, AT_BN + i], consts[D:P, AT_BN + i] = bh[P:3 * D], bi[P:3 * D]
    consts[D:P, AT_W2:AT_W2 + D] = L0_gnn_W2
    consts[0:D, AT_WT:AT_WT + D] = np.asarray(L1_gnn_weight).T
    w1 = np.zeros((P, P), np.float32)
    w1[0:D, 0:D] = w1[D:P, D:P] = L0_gnn_W1
    arrays = {
        "adj_t": adj_t,
        "x_t": np.ascontiguousarray(np.asarray(x).T),
        "x_pairs": np.ascontiguousarray(
            np.asarray(x).T.reshape(D, NCH, 2, 2 * P).transpose(2, 0, 1, 3)).reshape(P, N // 2),
        "w1": w1,
        "consts": consts,
        "bias": np.ascontiguousarray(L1_gnn_bias).reshape(1, D),
    }
    nc = bacc.Bacc("TRN2", target_bir_lowering=False, num_devices=1, dynamic_dma_scratch_size=1024)
    aps = {name: nc.dram_tensor(f"in_{name}", a.shape, mybir.dt.from_np(a.dtype),
                                kind="ExternalInput").ap() for name, a in arrays.items()}
    out = nc.dram_tensor("out_nodes", (N, D), F32, kind="ExternalOutput").ap()
    h_dram = nc.dram_tensor("h_dram", (D, N), F32, kind="Internal").ap()
    aps["bias"] = aps["bias"].unsqueeze(1).to_broadcast([P, KT, D])
    build(nc, out=out.rearrange("(c k p) d -> c p k d", k=KT, p=P), h_dram=h_dram, **aps)
    r = run_bass_kernel_spmd(nc, [{f"in_{name}": a for name, a in arrays.items()}], core_ids=[0])
    return r.results[0]["out_nodes"]
```
